# Optimizing a Trainium2 kernel written in Bass

```python
import numpy as np
import jax
import jax.numpy as jnp

def _softmax(x, axis=-1):
    return jax.nn.softmax(x, axis=axis)

def _gelu(x):
    return jax.nn.gelu(x, approximate=True)

def _silu(x):
    return jax.nn.silu(x)

def _sigmoid(x):
    return jax.nn.sigmoid(x)

def _layernorm(x, axis=-1, eps=1e-05):
    m = jnp.mean(x, axis=axis, keepdims=True)
    v = jnp.var(x, axis=axis, keepdims=True)
    return (x - m) / jnp.sqrt(v + eps)

def _scatter_add(tgt, idx, src, axis=0):
    return tgt.at[idx].add(src)

def _segment_sum(src, seg, n):
    return jax.ops.segment_sum(src, seg, n)
kernel_name = 'mk_gnn_preln_d2_gnn_r8_a18b32'

def setup_inputs(seed: int=0):
    np.random.seed(seed)
    _w = jnp.asarray

    def _rec_inputs():
        import jax
        import jax.numpy as jnp
        _gk = jax.random.key(seed)
        x = -0.0005121 + 1.001 * jax.random.normal(jax.random.fold_in(_gk, 1), (6250, 64), jnp.float32)
        src = jax.random.randint(jax.random.fold_in(_gk, 2), (200000,), 0, 6250, jnp.int32)
        dst = jax.random.randint(jax.random.fold_in(_gk, 3), (200000,), 0, 6250, jnp.int32)
        _o = jnp.argsort(dst, stable=True)
        src = src[_o]
        dst = dst[_o]
        edge_attr_16 = 0.000254156 + 0.999948 * jax.random.normal(jax.random.fold_in(_gk, 11), (200000, 16), jnp.float32)
        return (x, src, dst, edge_attr_16)
    x, src, dst, edge_attr_16 = _rec_inputs()

    def _L0_gnn_setup():
        import jax, jax.numpy as jnp
        import numpy as np
        N = 6250
        E = 100000
        D = 64
        EDGE_DIM = 16
        L = 3
        MSG_IN = 2 * D + EDGE_DIM
        UPD_IN = D + D
        key = jax.random.key(seed)
        ks = jax.random.split(key, 8)
        x = jax.random.normal(ks[0], (N, D), dtype=jnp.float32)
        edge_index = jax.random.randint(ks[1], (2, E), 0, N, dtype=jnp.int64)
        edge_attr = jax.random.normal(ks[2], (E, EDGE_DIM), dtype=jnp.float32)
        sc_m = 1.0 / np.sqrt(MSG_IN)
        sc_u = 1.0 / np.sqrt(UPD_IN)
        msg_w = jax.random.uniform(ks[3], (L, MSG_IN, D), jnp.float32, -sc_m, sc_m)
        msg_b = jax.random.uniform(ks[4], (L, D), jnp.float32, -sc_m, sc_m)
        upd_w = jax.random.uniform(ks[5], (L, UPD_IN, D), jnp.float32, -sc_u, sc_u)
        upd_b = jax.random.uniform(ks[6], (L, D), jnp.float32, -sc_u, sc_u)
        return {'x': x, 'edge_index': edge_index, 'edge_attr': edge_attr, 'msg_w': msg_w, 'msg_b': msg_b, 'upd_w': upd_w, 'upd_b': upd_b}
    _L0_gnn_all = _L0_gnn_setup()
    _L0_gnn_in = {k: v for k, v in _L0_gnn_all.items() if k in ('msg_w', 'msg_b', 'upd_w', 'upd_b')}
    del _L0_gnn_all

    def _L1_gnn_setup():
        import jax, jax.numpy as jnp
        import numpy as np
        EPS = 1e-07
        key = jax.random.key(seed)
        ks = jax.random.split(key, 6)
        N, E, D, H = (6250, 100000, 64, 128)
        x = jax.random.normal(ks[0], (N, D), dtype=jnp.float32)
        edge_index = jax.random.randint(ks[1], (2, E), 0, N, dtype=jnp.int64)
        W1 = jax.random.normal(ks[2], (D, H), dtype=jnp.float32) * (1.0 / np.sqrt(D))
        b1 = jnp.zeros((H,), dtype=jnp.float32)
        W2 = jax.random.normal(ks[3], (H, D), dtype=jnp.float32) * (1.0 / np.sqrt(H))
        b2 = jnp.zeros((D,), dtype=jnp.float32)
        t = jnp.ones((1,), dtype=jnp.float32)
        return {'x': x, 'edge_index': edge_index, 'W1': W1, 'b1': b1, 'W2': W2, 'b2': b2, 't': t}
    _L1_gnn_all = _L1_gnn_setup()
    _L1_gnn_in = {k: v for k, v in _L1_gnn_all.items() if k in ('W1', 'b1', 'W2', 'b2', 't')}
    del _L1_gnn_all
    return {'x': x, 'src': src, 'dst': dst, 'edge_attr_16': edge_attr_16, 'L0_gnn_msg_w': _L0_gnn_in['msg_w'], 'L0_gnn_msg_b': _L0_gnn_in['msg_b'], 'L0_gnn_upd_w': _L0_gnn_in['upd_w'], 'L0_gnn_upd_b': _L0_gnn_in['upd_b'], 'L1_gnn_W1': _L1_gnn_in['W1'], 'L1_gnn_b1': _L1_gnn_in['b1'], 'L1_gnn_W2': _L1_gnn_in['W2'], 'L1_gnn_b2': _L1_gnn_in['b2'], 'L1_gnn_t': _L1_gnn_in['t']}

def reference(x, src, dst, edge_attr_16, L0_gnn_msg_w, L0_gnn_msg_b, L0_gnn_upd_w, L0_gnn_upd_b, L1_gnn_W1, L1_gnn_b1, L1_gnn_W2, L1_gnn_b2, L1_gnn_t):
    import jax
    import jax.numpy as jnp

    def _L0_gnn_ref(x, edge_index, edge_attr, msg_w, msg_b, upd_w, upd_b):
        import jax, jax.numpy as jnp
        import numpy as np
        N = 6250
        E = 100000
        D = 64
        EDGE_DIM = 16
        L = 3
        MSG_IN = 2 * D + EDGE_DIM
        UPD_IN = D + D
        src = edge_index[0]
        dst = edge_index[1]
        n = x.shape[0]
        num_layers = msg_w.shape[0]
        for l in range(num_layers):
            x_i = x[dst]
            x_j = x[src]
            m_in = jnp.concatenate([x_i, x_j, edge_attr], axis=1)
            m = jax.nn.relu(m_in @ msg_w[l] + msg_b[l])
            agg = jax.ops.segment_sum(m, dst, num_segments=n)
            u_in = jnp.concatenate([x, agg], axis=1)
            x = jax.nn.relu(u_in @ upd_w[l] + upd_b[l])
        return x

    def _L1_gnn_ref(x, edge_index, W1, b1, W2, b2, t):
        import jax, jax.numpy as jnp
        import numpy as np
        EPS = 1e-07
        N = x.shape[0]
        src, dst = (edge_index[0], edge_index[1])
        msg = jax.nn.relu(x[src]) + EPS
        logits = msg * t
        seg_max = jax.ops.segment_max(logits, dst, num_segments=N)
        seg_max = jnp.where(jnp.isfinite(seg_max), seg_max, 0.0)
        e = jnp.exp(logits - seg_max[dst])
        denom = jax.ops.segment_sum(e, dst, num_segments=N)
        w = e / denom[dst]
        agg = jax.ops.segment_sum(msg * w, dst, num_segments=N)
        out = agg + x
        h = jax.nn.relu(out @ W1 + b1)
        return h @ W2 + b2
    edge_index = jnp.stack([src, dst])
    h = jnp.maximum(_layernorm(x, axis=-1), 0.0)
    x = x + _L0_gnn_ref(h, edge_index, edge_attr_16, L0_gnn_msg_w, L0_gnn_msg_b, L0_gnn_upd_w, L0_gnn_upd_b)
    h = jnp.maximum(_layernorm(x, axis=-1), 0.0)
    x = x + _L1_gnn_ref(h, edge_index, L1_gnn_W1, L1_gnn_b1, L1_gnn_W2, L1_gnn_b2, L1_gnn_t)
    return x

_drawn_inputs = setup_inputs


def setup_inputs(seed=0):
    import zlib

    import numpy as np

    out = dict(_drawn_inputs(seed))
    spreads = {'L1_gnn_b1': (0.0, 2.0), 'L1_gnn_b2': (0.0, 0.8)}
    factors = {'L0_gnn_upd_b': 3.138}
    for name, (base, spread) in spreads.items():
        noise = np.random.default_rng([zlib.crc32(name.encode()), seed]).standard_normal(out[name].shape)
        drawn = base * np.exp(spread * noise) if base else spread * noise
        out[name] = jnp.asarray(drawn.astype(out[name].dtype))
    for name, factor in factors.items():
        out[name] = (out[name] * factor).astype(out[name].dtype)
    return out
```

```python
from contextlib import ExitStack

import concourse.bass as bass
from concourse import mybir

P = 128
N = 6250
D = 64
ED = 16
E = 200000
LAYERS = 3
H1 = 128
NT = -(-N // P)
NP = NT * P
K = 4
UE = P * K
TURNS = -(-E // (2 * UE * 4))
UNITS = 4 * TURNS
HALF = UNITS * UE
EP = 2 * HALF
ROW = 512
ROWS = EP // ROW
KEEP_W = EP // P
GROUPS = [(c, min(4, NT - c)) for c in range(0, NT, 4)]
NG = len(GROUPS)
START_ROWS = EP + NP
ZW = START_ROWS * D // P // 64
EPS_LN = 1e-5
EPS_MSG = 1e-7
FAR = 1.0e38
CREDIT = 4

F32 = mybir.dt.float32
I32 = mybir.dt.int32
U8 = mybir.dt.uint8
ALU = mybir.AluOpType
ACT = mybir.ActivationFunctionType
AX = mybir.AxisListType
assert START_ROWS * D == P * 64 * ZW and ZW <= 2 * 2 * K * 2 * D


def done(w):
    return w + 1 + CREDIT


def freed(w, slots):
    return w - slots + 1 + CREDIT


def build(nc, x, src, dst, dst_before, dst_last, attr, msg_w, msg_b, upd_w, upd_b, w1, b1, w2, b2, t, out):
    with ExitStack() as ctx:
        def sb(name, shape, dt=F32):
            return ctx.enter_context(nc.sbuf_tensor(name, shape, dt))

        def ps(name):
            return [ctx.enter_context(nc.psum_tensor(f"{name}{i}", [P, 512], F32)) for i in range(2)]

        def sem(name):
            return ctx.enter_context(nc.semaphore(name))

        table = nc.dram_tensor("table", (NP, D), F32).ap()
        start_rows = nc.dram_tensor("start_rows", (START_ROWS, D), F32).ap()
        sums = nc.dram_tensor("sums", (EP, D), F32).ap()
        numden = nc.dram_tensor("numden", (EP, 2 * D), F32).ap()
        maxima = nc.dram_tensor("maxima", (D, HALF), F32).ap()
        keep_d = nc.dram_tensor("keep_d", (EP,), U8).ap()
        bounds_d = nc.dram_tensor("bounds_d", (NP + 1,), F32).ap()
        seam_max_d = nc.dram_tensor("seam_max_d", (2, D), F32).ap()

        keep = sb("keep", [P, HALF], U8)
        nodes = sb("nodes", [P, NT, 2 * D])
        big = sb("big", [P, NT * 2 * D])
        ab = big[:, :].rearrange("p (c f) -> p c f", c=NT)
        res = sb("res", [P, NT, D])
        G = sb("G", [P, 4, K, 2, D])
        V = sb("V", [P, 2, K, 2, D])
        At = sb("At", [2 * ED, 2, UE])
        So = sb("So", [P, 2, 2 * K * 2 * D])
        afill = sb("afill", [P, 2, UE])
        pre = sb("pre", [P, 2, UE])
        m = sb("m", [P, 2, UE])
        sT = sb("sT", [P, 2, UE])
        idx = sb("idx", [P, 4, 2 * K], I32)
        wij = sb("wij", [D, 2 * D])
        wc = sb("wc", [2 * ED, 2 * D])
        wu = sb("wu", [2 * D, D])
        mb_row = sb("mb_row", [1, 2 * D])
        ub_row = sb("ub_row", [1, D])
        w1_sb = sb("w1_sb", [D, H1])
        w2_sb = sb("w2_sb", [H1, D])
        b1_col = sb("b1_col", [H1, 1])
        b2_row = sb("b2_row", [1, D])
        t_col = sb("t_col", [P, 1])
        ident = sb("ident", [P, P])
        ones = sb("ones", [1, P])
        ones_w = pre[:, 1, 0:ROWS]
        node_i = sb("node_i", [P, NT], I32)
        node_f = sb("node_f", [P, NT])
        row_f = sb("row_f", [P, NT])
        row_i = sb("row_i", [P, NT], I32)
        upto = sb("upto", [P, NT])
        before = sb("before", [P, NT])
        has = sb("has", [P, NT])
        cross = sb("cross", [P, NT])
        tmp = sb("tmp", [P, NT])
        start_i = sb("start_i", [P, NT], I32)
        end_i = sb("end_i", [P, NT], I32)
        seam_part = sb("seam_part", [P, 2])
        seam_all = sb("seam_all", [P, 2])
        seam_i = sb("seam_i", [P, 2], I32)
        seam_row = sb("seam_row", [P, D])
        seam_sum = sb("seam_sum", [P, 2 * D])
        seam_max = G[:, 1].rearrange("p k h f -> p (k h) f")[:, 0:2, :]
        seam_col = sb("seam_col", [D, 1])
        seam_f = G[:, 0].rearrange("p k h f -> p (k h) f")[:, 0:3, :]
        mean = sb("mean", [P, NT])
        var = sb("var", [P, NT])
        std = sb("std", [P, NT])
        zero_col = sb("zero_col", [1, 1])

        psN, psB, psV, psS = ps("psN"), ps("psB"), ps("psV"), ps("psS")

        HB = NT * D
        def run_max(r, a, b):
            return big[:, r * HB + a:r * HB + b]
        def logit(r):
            return big[:, r * HB + 520:r * HB + 520 + UE]
        def expo(r):
            return big[:, r * HB + 1040:r * HB + 1040 + 2 * UE]
        def weighted(r):
            return big[:, r * HB + 2064:r * HB + 2064 + UE]

        x_loaded = sem("x_loaded")
        dst_loaded = sem("dst_loaded")
        last_loaded = sem("last_loaded")
        zero_ready = sem("zero_ready")
        cleared = sem("cleared")
        consts_ready = sem("consts_ready")
        ids_ready = sem("ids_ready")
        v_step = sem("v_step")
        rows_found = sem("rows_found")
        row_got = [sem(f"row_got{i}") for i in range(4)]
        row_counted = sem("row_counted")
        upto_ready = sem("upto_ready")
        bounds_stored = sem("bounds_stored")
        bounds_loaded = sem("bounds_loaded")
        seam_parts = sem("seam_parts")
        seam_reduced = sem("seam_reduced")
        index_ready = sem("index_ready")
        keep_ready = sem("keep_ready")
        keep_stored = sem("keep_stored")
        keep_loaded = sem("keep_loaded")
        var_ready = sem("var_ready")
        std_ready = sem("std_ready")
        h_ready = sem("h_ready")
        weights_loaded = sem("weights_loaded")
        mlp_loaded = sem("mlp_loaded")
        tab_turned = sem("tab_turned")
        tab_copied = sem("tab_copied")
        tab_mult = sem("tab_mult")
        ab_ready = sem("ab_ready")
        table_stored = sem("table_stored")
        scattered = sem("scattered")
        seam_got = sem("seam_got")
        seam_stored = sem("seam_stored")
        pool_turn = sem("pool_turn")
        pe_turn = sem("pe_turn")
        dve_turn = sem("dve_turn")
        idx_ready = [sem(f"idx_ready{j}") for j in range(4)]
        gathered = [sem(f"gathered{j}") for j in range(4)]
        attr_ready = [sem(f"attr_ready{j}") for j in range(2)]
        v_ready = [sem(f"v_ready{j}") for j in range(2)]
        v_turned = sem("v_turned")
        b_ready = sem("b_ready")
        filled = sem("filled")
        pre_ready = sem("pre_ready")
        m_ready = sem("m_ready")
        s_ready = sem("s_ready")
        s_turned = sem("s_turned")
        so_ready = sem("so_ready")
        s_stored = [sem(f"s_stored{j}") for j in range(2)]
        reset = sem("reset")
        agg_got = [sem(f"agg_got{g}") for g in range(NG)]
        seam_loaded = sem("seam_loaded")
        seam_spread = sem("seam_spread")
        masked = sem("masked")
        agg_ready = sem("agg_ready")
        upd_turned = sem("upd_turned")
        upd_copied = sem("upd_copied")
        upd_mult = sem("upd_mult")
        upd_done = sem("upd_done")
        msg_ready = sem("msg_ready")
        logit_ready = sem("logit_ready")
        pen_ready = sem("pen_ready")
        carry_ready = sem("carry_ready")
        max_ready = sem("max_ready")
        diff_ready = sem("diff_ready")
        exp_ready = sem("exp_ready")
        weighted_ready = sem("weighted_ready")
        den_ready = sem("den_ready")
        max_stored = [sem(f"max_stored{j}") for j in range(2)]
        seam_col_got = sem("seam_col_got")
        seam_cols_stored = sem("seam_cols_stored")
        seam_max_loaded = sem("seam_max_loaded")
        seam_diff = sem("seam_diff")
        seam_exp = sem("seam_exp")
        fin_turned = sem("fin_turned")
        fin_copied = sem("fin_copied")
        fin_hidden = sem("fin_hidden")
        fin_relu = sem("fin_relu")
        fin_mult = sem("fin_mult")
        fin_done = sem("fin_done")
        out_stored = sem("out_stored")

        src_u = src.rearrange("(u p k) -> u p k", p=P, k=2 * K)
        attr_u = attr.rearrange("c (u e) -> u c e", e=UE)
        start_u = start_rows[0:EP, :].rearrange("(h u p k) f -> h u p k f", h=2, p=P, k=K)
        sums_u = sums.rearrange("(h u p k) f -> h u p (k f)", h=2, p=P, k=K)
        numden_u = numden.rearrange("(h u p k) f -> h u p (k f)", h=2, p=P, k=K)
        max_u = maxima.rearrange("f (u e) -> u f e", e=UE)
        clear_v = start_rows.rearrange("(p r) f -> p (r f)", p=P).rearrange("p (a z) -> p a z", z=ZW)
        x_v = x.rearrange("(p c) f -> p c f", p=P)
        out_v = out.rearrange("(p c) f -> p c f", p=P)
        table_v = table.rearrange("(p c) f -> p c f", p=P)

        def by_k(tile, k):
            return tile.rearrange("c (p k) -> c k p", k=K)[:, k, :]

        block = ctx.enter_context(nc.Block())

        @block.sync
        def _(sp):
            sp.dma_start(big[:, 0:KEEP_W].bitcast(I32), dst.rearrange("(p e) -> p e", p=P)).then_inc(dst_loaded, 16)
            sp.dma_start(big[:, 2048:2048 + KEEP_W].bitcast(I32), dst_before.rearrange("(p e) -> p e", p=P)).then_inc(dst_loaded, 16)
            sp.dma_start(pre[:, 0, 0:ROWS].bitcast(I32), dst_last.partition_broadcast(P)).then_inc(last_loaded, 16)
            sp.dma_start(res[:, :, :], x_v).then_inc(x_loaded, 16)
            sp.dma_start(w1_sb[:, :], w1).then_inc(mlp_loaded, 16)
            sp.dma_start(w2_sb[:, :], w2).then_inc(mlp_loaded, 16)
            sp.dma_start(b1_col[:, :], b1.rearrange("(p a) -> p a", a=1)).then_inc(mlp_loaded, 16)
            sp.dma_start(b2_row[:, :], b2.rearrange("(a n) -> a n", a=1)).then_inc(mlp_loaded, 16)
            sp.dma_start(t_col[:, :], t.partition_broadcast(P)).then_inc(mlp_loaded, 16)
            sp.wait_ge(keep_ready, 1)
            sp.dma_start(keep_d.rearrange("(p e) -> p e", p=P), big[:, 4096:4096 + KEEP_W // 4].bitcast(U8)).then_inc(keep_stored, 16)
            sp.wait_ge(keep_stored, 16)
            for h in range(2):
                for q in range(4):
                    a, w = q * (HALF // 4), HALF // 4
                    sp.dma_start(keep[D * h:D * h + D, a:a + w],
                                 keep_d[h * HALF + a:h * HALF + a + w].partition_broadcast(D)).then_inc(keep_loaded, 16)
            sp.wait_ge(v_step, 1)
            sp.dma_start(bounds_d[0:1].rearrange("(a b) -> a b", a=1), zero_col[:, :]).then_inc(bounds_stored, 16)
            sp.wait_ge(upto_ready, 1)
            sp.dma_start(bounds_d[1:NP + 1].rearrange("(p c) -> p c", p=P), upto[:, :]).then_inc(bounds_stored, 16)
            sp.wait_ge(bounds_stored, 32)
            sp.dma_start(before[:, :], bounds_d[0:NP].rearrange("(p c) -> p c", p=P)).then_inc(bounds_loaded, 16)

            def load_idx(w, i, j):
                sp.wait_ge(b_ready, freed(w, 4))
                sp.dma_start(idx[:, j, :], src_u[i * 4 + j]).then_inc(idx_ready[j], 16)

            with sp.Fori(0, LAYERS) as l:
                sp.wait_ge(h_ready, l + 1)
                sp.dma_start(wij[:, 0:D], msg_w[l, 0:D, :]).then_inc(weights_loaded, 16)
                sp.dma_start(wij[:, D:2 * D], msg_w[l, D:2 * D, :]).then_inc(weights_loaded, 16)
                sp.dma_start(wc[0:ED, 0:D], msg_w[l, 2 * D:2 * D + ED, :]).then_inc(weights_loaded, 16)
                sp.dma_start(wc[ED:2 * ED, D:2 * D], msg_w[l, 2 * D:2 * D + ED, :]).then_inc(weights_loaded, 16)
                sp.dma_start(wu[:, :], upd_w[l, :, :]).then_inc(weights_loaded, 16)
                sp.dma_start(mb_row[:, 0:D], msg_b[bass.ds(l, 1), :]).then_inc(weights_loaded, 16)
                sp.dma_start(ub_row[:, :], upd_b[bass.ds(l, 1), :]).then_inc(weights_loaded, 16)
                sp.wait_ge(ab_ready, l * NG + NG)
                sp.dma_start(table_v, ab[:, :, D:2 * D]).then_inc(table_stored, 16)
                sp.wait_ge(seam_got, l * 16 + 16)
                sp.dma_start(start_rows[HALF:HALF + 1, :], seam_row[0:1, :]).then_inc(seam_stored, 16)
                with sp.Fori(0, TURNS) as i:
                    for j in range(4):
                        w = (l * TURNS + i) * 4 + j
                        load_idx(w, i, j)
                        sp.wait_ge(b_ready, freed(w, 2))
                        sp.dma_start(At[:, j % 2, :], attr_u[i * 4 + j]).then_inc(attr_ready[j % 2], 16)
                        sp.wait_ge(seam_stored, l * 16 + 16)
                        sp.wait_ge(v_turned, freed(w, 2))
                        for h in range(2):
                            sp.dma_start(V[:, j % 2, :, h, :], start_u[h, i * 4 + j]).then_inc(v_ready[j % 2], 16)
                for r in range(2):
                    sp.wait_ge(s_stored[r], l * (64 * TURNS) + (64 * TURNS + 32))
                sp.dma_start(seam_sum[:, 0:D], sums[HALF - 1, :].partition_broadcast(P)).then_inc(seam_loaded, 16)

            sp.wait_ge(msg_ready, 1)
            sp.dma_start(table_v, ab[:, :, 0:D]).then_inc(table_stored, 16)
            with sp.Fori(0, TURNS) as i:
                for j in range(4):
                    load_idx((i + LAYERS * TURNS) * 4 + j, i, j)
            W = (LAYERS + 1) * UNITS
            for r in range(2):
                sp.wait_ge(s_stored[r], 32 * (1 + W // 2))
                sp.wait_ge(max_stored[r], 16 * (1 + UNITS // 2))
            sp.dma_start(seam_sum[:, :], numden[HALF - 1, :].partition_broadcast(P)).then_inc(seam_loaded, 16)
            column = sp.value_load(seam_i[0:1, 1:2], min_val=0, max_val=HALF - 1)
            sp.dma_start(seam_col[:, :], maxima[:, bass.ds(column, 1)],
                         allow_slow_non_contiguous=True).then_inc(seam_col_got, 16)
            sp.dma_start(seam_max_d[0, :].rearrange("(f a) -> f a", a=1),
                         run_max(1, UE, UE + 1)[0:D, :]).then_inc(seam_cols_stored, 16)
            sp.wait_ge(seam_col_got, 16)
            sp.dma_start(seam_max_d[1, :].rearrange("(f a) -> f a", a=1), seam_col[:, :]).then_inc(seam_cols_stored, 16)
            sp.wait_ge(seam_cols_stored, 32)
            sp.dma_start(seam_max[:, :, :], seam_max_d.partition_broadcast(P)).then_inc(seam_max_loaded, 16)
            for g, (c, n) in enumerate(GROUPS):
                sp.wait_ge(fin_done, g + 1)
                sp.dma_start(out_v[:, c:c + n, :], res[:, c:c + n, :]).then_inc(out_stored, 16)
            sp.wait_ge(out_stored, 16 * NG)

        @block.gpsimd
        def _(pool):
            pool.iota(node_i[:, :], pattern=[[1, NT]], base=0, channel_multiplier=NT).then_inc(ids_ready, 1)
            pool.memset(ident[:, :], 0.0).then_inc(ids_ready, 1)
            pool.wait_ge(ids_ready, 2)
            pool.affine_select(out=ident[:, :], in_=ident[:, :], compare_op=ALU.not_equal, fill=1.0, base=0,
                               pattern=[[-1, P]], channel_multiplier=1).then_inc(consts_ready, 1)

            pool.wait_ge(rows_found, 1)
            dst_rows = dst.rearrange("(a b) -> a b", b=ROW)
            for c in range(NT):
                if c >= 4:
                    pool.wait_ge(row_counted, c - 3)
                pool.indirect_dma_start(
                    out=G[:, c % 4].rearrange("p k h f -> p (k h f)").bitcast(I32), out_offset=None, in_=dst_rows,
                    in_offset=bass.IndirectOffsetOnAxis(ap=row_i[:, c:c + 1], axis=0)).then_inc(row_got[c % 4], 16)
            pool.wait_ge(seam_parts, 1)
            pool.partition_all_reduce(seam_all[:, :], seam_part[:, :], P, bass.bass_isa.ReduceOp.add).then_inc(seam_reduced, 1)
            pool.wait_ge(index_ready, 2)
            pool.wait_ge(cleared, 16 * 2)
            for r in range(2):
                pool.wait_ge(max_stored[r], 16)
                pool.wait_ge(s_stored[r], 32)

            def fetch(w, j):
                pool.wait_ge(idx_ready[j], (w - j) * 4 + 16)
                pool.sem_inc(pool_turn, 1)
                for k in range(K):
                    for h in range(2):
                        pool.indirect_dma_start(
                            out=G[:, j, k, h, :], out_offset=None, in_=table,
                            in_offset=bass.IndirectOffsetOnAxis(ap=idx[:, j, 2 * k + h:2 * k + h + 1], axis=0))\
                            .then_inc(gathered[j], 16)

            with pool.Fori(0, LAYERS) as l:
                for g, (c0, n) in enumerate(GROUPS):
                    pool.wait_ge(ab_ready, l * NG + g + 1)
                    pool.sem_inc(pool_turn, 1)
                    for c in range(c0, c0 + n):
                        pool.indirect_dma_start(
                            out=start_rows, out_offset=bass.IndirectOffsetOnAxis(ap=start_i[:, c:c + 1], axis=0),
                            in_=ab[:, c, 0:D], in_offset=None).then_inc(scattered, 16)
                pool.wait_ge(scattered, l * (16 * NT) + 16 * NT)
                pool.sem_inc(pool_turn, 1)
                pool.indirect_dma_start(
                    out=seam_row[:, :], out_offset=None, in_=start_rows,
                    in_offset=bass.IndirectOffsetOnAxis(ap=seam_i[:, 0:1], axis=0)).then_inc(seam_got, 16)
                pool.wait_ge(table_stored, l * 16 + 16)
                pool.sem_inc(pool_turn, 1)
                with pool.Fori(0, TURNS) as i:
                    for j in range(4):
                        fetch((l * TURNS + i) * 4 + j, j)
                for r in range(2):
                    pool.wait_ge(s_stored[r], l * (64 * TURNS) + (64 * TURNS + 32))
                pool.sem_inc(pool_turn, 1)
                for g, (c0, n) in enumerate(GROUPS):
                    for c in range(c0, c0 + n):
                        pool.indirect_dma_start(
                            out=nodes[:, c, D:2 * D], out_offset=None, in_=sums,
                            in_offset=bass.IndirectOffsetOnAxis(ap=end_i[:, c:c + 1], axis=0)).then_inc(agg_got[g], 16)
            pool.wait_ge(table_stored, 16 * (LAYERS + 1))
            with pool.Fori(0, TURNS) as i:
                for j in range(4):
                    fetch((i + LAYERS * TURNS) * 4 + j, j)
            W = (LAYERS + 1) * UNITS
            for r in range(2):
                pool.wait_ge(s_stored[r], 32 * (1 + W // 2))
                pool.wait_ge(max_stored[r], 16 * (1 + UNITS // 2))
            pool.wait_ge(seam_cols_stored, 32)
            for g, (c0, n) in enumerate(GROUPS):
                for c in range(c0, c0 + n):
                    pool.indirect_dma_start(
                        out=ab[:, c, :], out_offset=None, in_=numden,
                        in_offset=bass.IndirectOffsetOnAxis(ap=end_i[:, c:c + 1], axis=0)).then_inc(agg_got[g], 16)

        @block.scalar
        def _(act):
            act.wait_ge(zero_ready, 1)
            zeros = So[:, :, :].rearrange("p r f -> p (r f)")[:, 0:ZW].unsqueeze(1)
            for q in range(8):
                s = s_stored[q % 2] if q < 4 else max_stored[q % 2] if q < 6 else cleared
                act.dma_start(clear_v[:, 8 * q:8 * q + 8, :], zeros.broadcast_to([P, 8, ZW])).then_inc(s, 16)
            for s in (m_ready, so_ready, logit_ready, pen_ready, exp_ready):
                act.sem_inc(s, CREDIT)
            act.wait_ge(var_ready, 1)
            nc.scalar.activation(std[:, :], var[:, :], ACT.Sqrt).then_inc(std_ready, 1)

            def store_slot(w, j):
                act.wait_ge(s_stored[j % 2], (w - j) * 16 + 32 * (j // 2) + 32)

            with act.Fori(0, LAYERS) as l:
                for g, (c0, n) in enumerate(GROUPS):
                    act.wait_ge(tab_turned, l * NG + g + 1)
                    if g >= 2:
                        act.wait_ge(tab_mult, l * NG + g - 1)
                    nc.scalar.activation(V[:, g % 2].rearrange("p k h f -> p (k h f)")[0:D, 0:n * P], psN[g % 2][0:D, 0:n * P],
                                         ACT.Copy).then_inc(tab_copied, 1)
                with act.Fori(0, TURNS) as i:
                    for j in range(4):
                        w, r = (l * TURNS + i) * 4 + j, j % 2
                        act.wait_ge(pre_ready, done(w))
                        act.wait_ge(s_ready, freed(w, 2))
                        nc.scalar.activation(m[:, r, :], pre[:, r, :], ACT.Relu).then_inc(m_ready, 1)
                        act.wait_ge(s_turned, done(w))
                        store_slot(w, j)
                        rows = So[:, r, 0:2 * K * D].rearrange("p (h k f) -> p k h f", h=2, k=K)
                        nc.scalar.activation(rows, psS[r][:, :].rearrange("p (k h f) -> p k h f", k=K, h=2),
                                             ACT.Copy).then_inc(so_ready, 1)
                        act.wait_ge(so_ready, done(w))
                        for h in range(2):
                            act.dma_start(sums_u[h, i * 4 + j], So[:, r, h * K * D:(h + 1) * K * D]).then_inc(s_stored[r], 16)
                for g, (c0, n) in enumerate(GROUPS):
                    act.wait_ge(upd_turned, l * NG + g + 1)
                    if g >= 2:
                        act.wait_ge(upd_mult, l * NG + g - 1)
                    nc.scalar.activation(V[:, g % 2].rearrange("p k h f -> p (k h f)")[:, 0:n * P], psN[g % 2][:, 0:n * P],
                                         ACT.Copy).then_inc(upd_copied, 1)
            act.wait_ge(var_ready, 2)
            nc.scalar.activation(std[:, :], var[:, :], ACT.Sqrt).then_inc(std_ready, 1)
            act.wait_ge(mlp_loaded, 80)
            with act.Fori(0, TURNS) as i:
                for j in range(4):
                    w, r = (i + LAYERS * TURNS) * 4 + j, j % 2
                    v = i * 4 + j
                    act.wait_ge(b_ready, done(w))
                    act.wait_ge(diff_ready, freed(v, 2))
                    nc.scalar.activation(logit(r), psB[r][:, :], ACT.Copy, scale=t_col[:, 0:1]).then_inc(logit_ready, 1)
                    nc.scalar.activation(pre[:, r, :], keep[:, bass.ds((i * 4 + j) * UE, UE)], ACT.Copy,
                                         scale=FAR, bias=-FAR).then_inc(pen_ready, 1)
                    act.wait_ge(max_ready, done(v))
                    act.dma_start(max_u[i * 4 + j], run_max(r, 1, UE + 1)[D:2 * D, :]).then_inc(max_stored[r], 16)
                    act.wait_ge(diff_ready, done(v))
                    nc.scalar.activation(expo(r), expo(r), ACT.Exp).then_inc(exp_ready, 1)
                    act.wait_ge(s_turned, done(w))
                    store_slot(w, j)
                    rows = So[:, r, :].rearrange("p (h k q f) -> p q k h f", h=2, k=K, q=2)
                    for q, bank in ((0, psS[r]), (1, psV[r])):
                        ins = nc.scalar.activation(rows[:, q], bank[:, :].rearrange("p (k h f) -> p k h f", k=K, h=2), ACT.Copy)
                    ins.then_inc(so_ready, 1)
                    act.wait_ge(so_ready, done(w))
                    for h in range(2):
                        act.dma_start(numden_u[h, i * 4 + j], So[:, r, h * K * 2 * D:(h + 1) * K * 2 * D]).then_inc(s_stored[r], 16)
            act.wait_ge(seam_diff, 1)
            nc.scalar.activation(seam_f[:, 0:2, :], seam_max[:, :, :], ACT.Exp).then_inc(seam_exp, 1)
            for g, (c0, n) in enumerate(GROUPS):
                act.wait_ge(fin_turned, g + 1)
                if g >= 2:
                    act.wait_ge(fin_hidden, g - 1)
                nc.scalar.activation(V[:, g % 2].rearrange("p k h f -> p (k h f)")[0:D, 0:n * P], psN[g % 2][0:D, 0:n * P],
                                     ACT.Copy).then_inc(fin_copied, 1)
                act.wait_ge(fin_hidden, g + 1)
                if g >= 2:
                    act.wait_ge(fin_mult, g - 1)
                nc.scalar.activation(m[:, g % 2, 0:n * P], psB[g % 2][:, 0:n * P], ACT.Relu, bias=b1_col[:, 0:1])\
                    .then_inc(fin_relu, 1)

        @block.tensor
        def _(pe):
            for s in (v_turned, b_ready, s_turned):
                pe.sem_inc(s, CREDIT)
            pe.wait_ge(consts_ready, 1)

            def turn_nodes(g, turned, copied, base):
                c0, n = GROUPS[g]
                if g >= 2:
                    pe.wait_ge(copied, base + g - 1)
                for c in range(n):
                    ins = pe.transpose(psN[g % 2][:, c * P:(c + 1) * P], nodes[:, c0 + c, :], ident[:, :])
                ins.then_inc(turned, 1)

            def column_tile(g):
                return V[:, g % 2].rearrange("p k h f -> p (k h f)")

            with pe.Fori(0, LAYERS) as l:
                pe.wait_ge(h_ready, l + 1)
                pe.wait_ge(v_step, 2)
                turn_nodes(0, tab_turned, tab_copied, l * NG)
                for g, (c0, n) in enumerate(GROUPS):
                    if g + 1 < NG:
                        turn_nodes(g + 1, tab_turned, tab_copied, l * NG)
                    if g == 0:
                        pe.wait_ge(weights_loaded, l * 112 + 112)
                    pe.wait_ge(tab_copied, l * NG + g + 1)
                    if g >= 2:
                        pe.wait_ge(ab_ready, l * NG + g - 1)
                    for c in range(n):
                        o = psB[g % 2][:, c * P:(c + 1) * P]
                        pe.matmul(o, column_tile(g)[0:D, c * P:(c + 1) * P], wij[:, :], start=True, stop=False)
                        ins = pe.matmul(o, ones[0:1, :], mb_row[0:1, :], start=False, stop=True)
                    ins.then_inc(tab_mult, 1)
                pe.wait_ge(ab_ready, l * NG + NG)
                pe.sem_inc(pe_turn, 1)
                with pe.Fori(0, TURNS) as i:
                    for j in range(4):
                        w, r = (l * TURNS + i) * 4 + j, j % 2
                        pe.wait_ge(v_ready[r], (w - j) * 16 + 32 * (j // 2) + 32)
                        pe.wait_ge(filled, freed(w, 2))
                        for k in range(K):
                            ins = pe.transpose(by_k(psV[r][:, :], k), V[:, r, k].rearrange("p h f -> p (h f)"), ident[:, :])
                        ins.then_inc(v_turned, 1)
                        pe.wait_ge(attr_ready[r], (w - j) * 8 + 16 * (j // 2) + 16)
                        pe.wait_ge(pre_ready, freed(w, 2))
                        pe.matmul(psB[r][:, :], wc[:, :], At[:, r, :], start=True, stop=False)
                        pe.wait_ge(gathered[j], (w - j) * 32 + 128)
                        for k in range(K):
                            ins = pe.matmul(by_k(psB[r][:, :], k), G[:, j, k].rearrange("p h f -> p (h f)"), ident[:, :],
                                            start=False, stop=(k == K - 1))
                        ins.then_inc(b_ready, 1)
                        pe.wait_ge(s_ready, done(w))
                        pe.wait_ge(so_ready, freed(w, 2))
                        for k in range(K):
                            ins = pe.transpose(psS[r][:, k * P:(k + 1) * P], by_k(sT[:, r, :], k), ident[:, :])
                        ins.then_inc(s_turned, 1)
                for g in range(NG):
                    if g == 0:
                        pe.wait_ge(agg_ready, l * NG + 1)
                        turn_nodes(0, upd_turned, upd_copied, l * NG)
                    if g + 1 < NG:
                        pe.wait_ge(agg_ready, l * NG + g + 2)
                        turn_nodes(g + 1, upd_turned, upd_copied, l * NG)
                    pe.wait_ge(upd_copied, l * NG + g + 1)
                    if g >= 2:
                        pe.wait_ge(upd_done, l * NG + g - 1)
                    for c in range(GROUPS[g][1]):
                        o = psB[g % 2][:, c * D:(c + 1) * D]
                        pe.matmul(o, column_tile(g)[:, c * P:(c + 1) * P], wu[:, :], start=True, stop=False)
                        ins = pe.matmul(o, ones[0:1, :], ub_row[0:1, :], start=False, stop=True)
                    ins.then_inc(upd_mult, 1)
            pe.wait_ge(upd_done, LAYERS * NG)
            with pe.Fori(0, TURNS) as i:
                for j in range(4):
                    w, r, v = (i + LAYERS * TURNS) * 4 + j, j % 2, i * 4 + j
                    pe.wait_ge(gathered[j], (w - j) * 32 + 128)
                    pe.wait_ge(weighted_ready, freed(v, 2))
                    pe.wait_ge(logit_ready, freed(v, 2))
                    for k in range(K):
                        ins = pe.transpose(by_k(psB[r][:, :], k), G[:, j, k].rearrange("p h f -> p (h f)"), ident[:, :])
                    ins.then_inc(b_ready, 1)
                    pe.wait_ge(s_ready, done(w))
                    pe.wait_ge(so_ready, freed(w, 2))
                    for tile, bank in ((sT, psS[r]), (afill, psV[r])):
                        for k in range(K):
                            ins = pe.transpose(bank[:, k * P:(k + 1) * P], by_k(tile[:, r, :], k), ident[:, :])
                    ins.then_inc(s_turned, 1)
            pe.wait_ge(mlp_loaded, 80)
            for g, (c0, n) in enumerate(GROUPS):
                if g == 0:
                    pe.wait_ge(agg_ready, LAYERS * NG + 1)
                    turn_nodes(0, fin_turned, fin_copied, 0)
                if g + 1 < NG:
                    pe.wait_ge(agg_ready, LAYERS * NG + g + 2)
                    turn_nodes(g + 1, fin_turned, fin_copied, 0)
                pe.wait_ge(fin_copied, g + 1)
                if g >= 2:
                    pe.wait_ge(fin_relu, g - 1)
                pe.matmul(psB[g % 2][:, 0:n * P], w1_sb[:, :], column_tile(g)[0:D, 0:n * P], start=True, stop=True)\
                    .then_inc(fin_hidden, 1)
                pe.wait_ge(fin_relu, g + 1)
                if g >= 2:
                    pe.wait_ge(fin_done, g - 1)
                for c in range(n):
                    o = psV[g % 2][:, c * D:(c + 1) * D]
                    pe.matmul(o, m[:, g % 2, c * P:(c + 1) * P], w2_sb[:, :], start=True, stop=False)
                    ins = pe.matmul(o, ones[0:1, :], b2_row[0:1, :], start=False, stop=True)
                ins.then_inc(fin_mult, 1)

        @block.vector
        def _(dve):
            steps = [0]

            def step(ins):
                steps[0] += 1
                ins.then_inc(v_step, 1)
                dve.wait_ge(v_step, steps[0])

            step(nc.vector.memset(zero_col[:, :], 0.0))
            step(nc.vector.memset(ones[:, :], 1.0))
            step(nc.vector.memset(ones_w, 1.0))
            step(nc.vector.memset(mb_row[:, :], 0.0))
            step(nc.vector.memset(wc[:, :], 0.0))
            nc.vector.memset(So[:, :, :], 0.0).then_inc(zero_ready, 1)
            for s in (filled, pre_ready, s_ready, carry_ready, max_ready, diff_ready, weighted_ready, den_ready):
                dve.sem_inc(s, CREDIT)

            dve.wait_ge(dst_loaded, 32)
            nc.vector.tensor_tensor(big[:, 4096:4096 + KEEP_W // 4].bitcast(U8), big[:, 0:KEEP_W].bitcast(I32),
                                    big[:, 2048:2048 + KEEP_W].bitcast(I32), ALU.is_equal).then_inc(keep_ready, 1)

            dve.wait_ge(ids_ready, 2)
            step(nc.vector.tensor_copy(node_f[:, :], node_i[:, :]))
            dve.wait_ge(last_loaded, 16)
            for c in range(NT):
                ins = nc.vector.scalar_tensor_tensor(
                    out=m[:, 0, 0:ROWS], in0=pre[:, 0, 0:ROWS].bitcast(I32), scalar=node_f[:, c:c + 1], in1=ones_w,
                    op0=ALU.is_le, op1=ALU.mult, accum_out=row_f[:, c:c + 1])
                step(ins)
            step(nc.vector.tensor_scalar(row_f[:, :], row_f[:, :], float(ROWS - 1), None, ALU.min))
            nc.vector.tensor_copy(row_i[:, :], row_f[:, :]).then_inc(rows_found, 1)

            def layer_norm(last):
                def wide(a):
                    return a[:, :].unsqueeze(2).broadcast_to([P, NT, D])
                lo, hi = nodes[:, :, 0:D], nodes[:, :, D:2 * D]
                step(nc.vector.tensor_reduce(mean[:, :], res[:, :, :], AX.X, ALU.add))
                step(nc.vector.tensor_scalar(mean[:, :], mean[:, :], 1.0 / D, None, ALU.mult))
                step(nc.vector.tensor_tensor(lo, res[:, :, :], wide(mean), ALU.subtract))
                step(nc.vector.tensor_tensor(hi, lo, lo, ALU.mult))
                step(nc.vector.tensor_reduce(var[:, :], hi, AX.X, ALU.add))
                nc.vector.tensor_scalar(var[:, :], var[:, :], 1.0 / D, EPS_LN, ALU.mult, ALU.add).then_inc(var_ready, 1)
                dve.wait_ge(std_ready, last)
                step(nc.vector.reciprocal(std[:, :], std[:, :]))
                step(nc.vector.tensor_tensor(lo, lo, wide(std), ALU.mult))
                return nc.vector.tensor_scalar(lo, lo, 0.0, None, ALU.max)

            dve.wait_ge(x_loaded, 16)
            layer_norm(1).then_inc(h_ready, 1)

            step(nc.vector.memset(sT[:, 0, :], 1.0))
            for c in range(NT):
                dve.wait_ge(row_got[c % 4], 16 * (c // 4 + 1))
                if c >= 2:
                    dve.wait_ge(row_counted, c - 1)
                nc.vector.scalar_tensor_tensor(
                    out=m[:, c % 2, :], in0=G[:, c % 4].rearrange("p k h f -> p (k h f)").bitcast(I32),
                    scalar=node_f[:, c:c + 1], in1=sT[:, 0, :],
                    op0=ALU.is_le, op1=ALU.mult, accum_out=upto[:, c:c + 1]).then_inc(row_counted, 1)
            dve.wait_ge(row_counted, NT)
            nc.vector.scalar_tensor_tensor(out=upto[:, :], in0=row_f[:, :], scalar=float(ROW), in1=upto[:, :],
                                           op0=ALU.mult, op1=ALU.add).then_inc(upto_ready, 1)
            dve.wait_ge(bounds_loaded, 16)
            dve.wait_ge(upto_ready, 1)
            tt, ts = nc.vector.tensor_tensor, nc.vector.tensor_scalar
            step(tt(has[:, :], upto[:, :], before[:, :], ALU.is_gt))
            step(ts(tmp[:, :], upto[:, :], -1.0, 0.0, ALU.add, ALU.max))
            step(nc.vector.tensor_copy(end_i[:, :], tmp[:, :]))
            step(ts(tmp[:, :], node_f[:, :], float(EP), None, ALU.add))
            step(tt(mean[:, :], before[:, :], tmp[:, :], ALU.subtract))
            step(tt(mean[:, :], mean[:, :], has[:, :], ALU.mult))
            step(tt(tmp[:, :], mean[:, :], tmp[:, :], ALU.add))
            nc.vector.tensor_copy(start_i[:, :], tmp[:, :]).then_inc(index_ready, 1)
            step(ts(mean[:, :], before[:, :], float(HALF), None, ALU.is_lt))
            step(ts(tmp[:, :], upto[:, :], float(HALF), None, ALU.is_gt))
            step(tt(cross[:, :], mean[:, :], tmp[:, :], ALU.mult))
            step(nc.vector.scalar_tensor_tensor(out=tmp[:, :], in0=before[:, :], scalar=-float(HALF), in1=cross[:, :],
                                                op0=ALU.add, op1=ALU.mult, accum_out=seam_part[:, 0:1]))
            step(nc.vector.scalar_tensor_tensor(out=tmp[:, :], in0=upto[:, :], scalar=-float(HALF + 1), in1=cross[:, :],
                                                op0=ALU.add, op1=ALU.mult, accum_out=seam_part[:, 1:2]))
            dve.sem_inc(seam_parts, 1)
            dve.wait_ge(seam_reduced, 1)
            step(ts(seam_all[:, 0:1], seam_all[:, 0:1], float(HALF), None, ALU.add))
            nc.vector.tensor_copy(seam_i[:, :], seam_all[:, :]).then_inc(index_ready, 1)

            def tiles(a, c0, n):
                return a[:, c0:c0 + n].unsqueeze(2).broadcast_to([P, n, D])

            with dve.Fori(0, LAYERS) as l:
                for g, (c0, n) in enumerate(GROUPS):
                    dve.wait_ge(tab_mult, l * NG + g + 1)
                    nc.vector.tensor_copy(ab[:, c0:c0 + n, :], psB[g % 2][:, 0:n * P].rearrange("p (c f) -> p c f", c=n))\
                        .then_inc(ab_ready, 1)
                nc.vector.memset(afill[:, 1, UE - 1:UE], 0.0).then_inc(reset, 1)
                nc.vector.memset(sT[:, 1, UE - 1:UE], 0.0).then_inc(reset, 1)
                dve.wait_ge(keep_loaded, 128)
                dve.wait_ge(reset, l * 2 + 2)
                dve.sem_inc(dve_turn, 1)
                with dve.Fori(0, TURNS) as i:
                    for j in range(4):
                        w, r = (l * TURNS + i) * 4 + j, j % 2
                        kept = keep[:, bass.ds((i * 4 + j) * UE, UE)]
                        dve.wait_ge(v_turned, done(w))
                        nc.vector.tensor_tensor_scan(afill[:, r, :], kept, psV[r][:, :], afill[:, 1 - r, UE - 1:UE],
                                                     ALU.mult, ALU.add).then_inc(filled, 1)
                        dve.wait_ge(filled, done(w))
                        dve.wait_ge(b_ready, done(w))
                        nc.vector.tensor_tensor(pre[:, r, :], afill[:, r, :], psB[r][:, :], ALU.add).then_inc(pre_ready, 1)
                        dve.wait_ge(m_ready, done(w))
                        dve.wait_ge(s_turned, freed(w, 2))
                        nc.vector.tensor_tensor_scan(sT[:, r, :], kept, m[:, r, :], sT[:, 1 - r, UE - 1:UE],
                                                     ALU.mult, ALU.add).then_inc(s_ready, 1)
                        dve.wait_ge(s_ready, done(w))
                dve.wait_ge(seam_loaded, l * 16 + 16)
                nc.vector.tensor_tensor(ab[:, :, 0:D], tiles(cross, 0, NT),
                                        seam_sum[:, 0:D].unsqueeze(1).broadcast_to([P, NT, D]), ALU.mult).then_inc(seam_spread, 1)
                dve.wait_ge(seam_spread, l + 1)
                for g, (c0, n) in enumerate(GROUPS):
                    agg = nodes[:, c0:c0 + n, D:2 * D]
                    dve.wait_ge(agg_got[g], l * (16 * n) + 16 * n)
                    tt(agg, agg, tiles(has, c0, n), ALU.mult).then_inc(masked, 1)
                    dve.wait_ge(masked, l * NG + g + 1)
                    tt(agg, agg, ab[:, c0:c0 + n, 0:D], ALU.add).then_inc(agg_ready, 1)
                for g, (c0, n) in enumerate(GROUPS):
                    dve.wait_ge(upd_mult, l * NG + g + 1)
                    ts(nodes[:, c0:c0 + n, 0:D], psB[g % 2][:, 0:n * D].rearrange("p (c f) -> p c f", c=n), 0.0, None,
                       ALU.max).then_inc(upd_done, 1)
                dve.wait_ge(upd_done, l * NG + NG)
                dve.sem_inc(h_ready, 1)

            step(tt(res[:, :, :], res[:, :, :], nodes[:, :, 0:D], ALU.add))
            step(layer_norm(2))
            nc.vector.tensor_scalar(ab[:, :, 0:D], nodes[:, :, 0:D], EPS_MSG, None, ALU.add).then_inc(msg_ready, 1)
            dve.wait_ge(table_stored, 16 * (LAYERS + 1))
            step(nc.vector.memset(run_max(1, UE, UE + 1), -FAR))
            step(nc.vector.memset(sT[:, 1, UE - 1:UE], 0.0))
            step(nc.vector.memset(afill[:, 1, UE - 1:UE], 0.0))
            with dve.Fori(0, TURNS) as i:
                for j in range(4):
                    w, r, v = (i + LAYERS * TURNS) * 4 + j, j % 2, i * 4 + j
                    dve.wait_ge(exp_ready, freed(v, 2))
                    nc.vector.tensor_copy(run_max(r, 0, 1), run_max(1 - r, UE, UE + 1)).then_inc(carry_ready, 1)
                    dve.wait_ge(carry_ready, done(v))
                    dve.wait_ge(pen_ready, done(v))
                    dve.wait_ge(max_stored[r], i * 32 + 16 * (j // 2) + 16)
                    nc.vector.tensor_tensor_scan(run_max(r, 1, UE + 1), pre[:, r, :], logit(r), run_max(r, 0, 1),
                                                 ALU.add, ALU.max).then_inc(max_ready, 1)
                    dve.wait_ge(max_ready, done(v))
                    tt(expo(r)[:, 0:UE], run_max(r, 0, UE), run_max(r, 1, UE + 1), ALU.subtract).then_inc(v_step, 1)
                    dve.wait_ge(v_step, steps[0] + (i * 4 + j) + 1)
                    tt(expo(r)[:, 0:UE], expo(r)[:, 0:UE], pre[:, r, :], ALU.add)
                    tt(expo(r)[:, UE:2 * UE], logit(r), run_max(r, 1, UE + 1), ALU.subtract).then_inc(diff_ready, 1)
                    dve.wait_ge(exp_ready, done(v))
                    tt(weighted(r), expo(r)[:, UE:2 * UE], psB[r][:, :], ALU.mult).then_inc(weighted_ready, 1)
                    dve.wait_ge(s_turned, freed(w, 2))
                    nc.vector.tensor_tensor_scan(afill[:, r, :], expo(r)[:, 0:UE], expo(r)[:, UE:2 * UE],
                                                 afill[:, 1 - r, UE - 1:UE], ALU.mult, ALU.add).then_inc(den_ready, 1)
                    dve.wait_ge(weighted_ready, done(v))
                    nc.vector.tensor_tensor_scan(sT[:, r, :], expo(r)[:, 0:UE], weighted(r),
                                                 sT[:, 1 - r, UE - 1:UE], ALU.mult, ALU.add).then_inc(s_ready, 1)
                    dve.wait_ge(den_ready, done(v))
                    dve.wait_ge(s_ready, done(w))

            steps[0] += UNITS
            dve.wait_ge(seam_max_loaded, 16)
            step(tt(seam_f[:, 2, :], seam_max[:, 0, :], seam_max[:, 1, :], ALU.max))
            tt(seam_max[:, :, :], seam_max[:, :, :], seam_f[:, 2, :].unsqueeze(1).broadcast_to([P, 2, D]),
               ALU.subtract).then_inc(seam_diff, 1)
            dve.wait_ge(seam_exp, 1)
            dve.wait_ge(seam_loaded, 16 * (LAYERS + 1))
            step(tt(seam_sum[:, :].rearrange("p (q f) -> p q f", q=2), seam_sum[:, :].rearrange("p (q f) -> p q f", q=2),
                    seam_f[:, 0, :].unsqueeze(1).broadcast_to([P, 2, D]), ALU.mult))
            step(ts(seam_f[:, 1, :], seam_f[:, 1, :], -1.0, None, ALU.add))

            def rows_of(a, n):
                return a.unsqueeze(1).broadcast_to([P, n, D])
            work = sT[:, :, :].rearrange("p r e -> p (r e)")
            for g, (c0, n) in enumerate(GROUPS):
                dve.wait_ge(agg_got[g], LAYERS * 16 * n + 16 * n)
                num, den = ab[:, c0:c0 + n, 0:D], ab[:, c0:c0 + n, D:2 * D]
                f1 = work[:, 0:n * D].rearrange("p (c f) -> p c f", c=n)
                add = work[:, 512:512 + n * D].rearrange("p (c f) -> p c f", c=n)
                step(tt(f1, tiles(cross, c0, n), rows_of(seam_f[:, 1, :], n), ALU.mult))
                step(ts(f1, f1, 1.0, None, ALU.add))
                for q, part in ((0, num), (1, den)):
                    step(tt(part, part, f1, ALU.mult))
                    step(tt(add, tiles(cross, c0, n), rows_of(seam_sum[:, q * D:(q + 1) * D], n), ALU.mult))
                    step(tt(part, part, add, ALU.add))
                step(nc.vector.reciprocal(den, den))
                step(tt(num, num, den, ALU.mult))
                step(tt(num, num, tiles(has, c0, n), ALU.mult))
                tt(nodes[:, c0:c0 + n, 0:D], nodes[:, c0:c0 + n, 0:D], num, ALU.add).then_inc(agg_ready, 1)
                if g >= 2:
                    dve.wait_ge(fin_mult, g - 1)
                    tt(res[:, c0 - 8:c0 - 4, :], res[:, c0 - 8:c0 - 4, :],
                       psV[g % 2][:, 0:4 * D].rearrange("p (c f) -> p c f", c=4), ALU.add).then_inc(fin_done, 1)
            for g in range(NG - 2, NG):
                c0, n = GROUPS[g]
                dve.wait_ge(fin_mult, g + 1)
                tt(res[:, c0:c0 + n, :], res[:, c0:c0 + n, :],
                   psV[g % 2][:, 0:n * D].rearrange("p (c f) -> p c f", c=n), ALU.add).then_inc(fin_done, 1)


def kernel(**inputs):
    import numpy as np
    import concourse.bacc as bacc
    from concourse.bass_utils import run_bass_kernel_spmd

    src = np.zeros((EP,), np.int32)
    src[:E] = inputs["src"]
    src = np.ascontiguousarray(src.reshape(2, UNITS, P, K).transpose(1, 2, 3, 0)).reshape(-1)
    dst = np.full((EP,), N, np.int32)
    dst[:E] = inputs["dst"]
    attr = np.zeros((EP, ED), np.float32)
    attr[:E] = inputs["edge_attr_16"]
    attr = np.ascontiguousarray(attr.reshape(2, HALF, ED).transpose(0, 2, 1)).reshape(2 * ED, HALF)
    x = np.zeros((NP, D), np.float32)
    x[:N] = inputs["x"]
    arrays = {
        "x": x, "src": src, "dst": dst, "dst_before": np.concatenate([np.full((1,), -1, np.int32), dst[:-1]]), "dst_last": dst[ROW - 1::ROW], "attr": attr,
        "msg_w": inputs["L0_gnn_msg_w"], "msg_b": inputs["L0_gnn_msg_b"],
        "upd_w": inputs["L0_gnn_upd_w"], "upd_b": inputs["L0_gnn_upd_b"],
        "w1": inputs["L1_gnn_W1"], "b1": inputs["L1_gnn_b1"], "w2": inputs["L1_gnn_W2"],
        "b2": inputs["L1_gnn_b2"], "t": inputs["L1_gnn_t"],
    }
    arrays = {k: np.ascontiguousarray(a) for k, a in arrays.items()}
    nc = bacc.Bacc("TRN2", target_bir_lowering=False, num_devices=1)
    args = [nc.dram_tensor(k, a.shape, mybir.dt.from_np(a.dtype), kind="ExternalInput").ap() for k, a in arrays.items()]
    out = nc.dram_tensor("out", (NP, D), F32, kind="ExternalOutput").ap()
    build(nc, *args, out)
    r = run_bass_kernel_spmd(nc, [arrays], core_ids=[0])
    return r.results[0]["out"][:N]
```

```python
from contextlib import ExitStack

import concourse.bass as bass
from concourse import mybir

P = 128
N = 6250
D = 64
ED = 16
E = 200000
LAYERS = 3
H1 = 128
NT = -(-N // P)
NP = NT * P
K = 4
UE = P * K
TURNS = -(-E // (2 * UE * 4))
UNITS = 4 * TURNS
HALF = UNITS * UE
EP = 2 * HALF
ROW = 512
ROWS = EP // ROW
KEEP_W = EP // P
GROUPS = [(c, min(4, NT - c)) for c in range(0, NT, 4)]
NG = len(GROUPS)
START_ROWS = EP + NP
ZW = START_ROWS * D // P // 64
EPS_LN = 1e-5
EPS_MSG = 1e-7
FAR = 1.0e38
WEIGHTS_CLEAR = 5
CREDIT = 4

F32 = mybir.dt.float32
I32 = mybir.dt.int32
U8 = mybir.dt.uint8
ALU = mybir.AluOpType
ACT = mybir.ActivationFunctionType
AX = mybir.AxisListType
assert START_ROWS * D == P * 64 * ZW and ZW <= 2 * 2 * K * 2 * D


def done(w):
    return w + 1 + CREDIT


def freed(w, slots):
    return w - slots + 1 + CREDIT


def build(nc, x, src, dst, dst_before, dst_last, attr, msg_w, msg_b, upd_w, upd_b, w1, b1, w2, b2, t, out):
    with ExitStack() as ctx:
        def sb(name, shape, dt=F32):
            return ctx.enter_context(nc.sbuf_tensor(name, shape, dt))

        def ps(name):
            return [ctx.enter_context(nc.psum_tensor(f"{name}{i}", [P, 512], F32)) for i in range(2)]

        def sem(name):
            return ctx.enter_context(nc.semaphore(name))

        table = nc.dram_tensor("table", (NP, D), F32).ap()
        start_rows = nc.dram_tensor("start_rows", (START_ROWS, D), F32).ap()
        sums = nc.dram_tensor("sums", (EP, D), F32).ap()
        numden = nc.dram_tensor("numden", (EP, 2 * D), F32).ap()
        maxima = nc.dram_tensor("maxima", (D, HALF), F32).ap()
        keep_d = nc.dram_tensor("keep_d", (EP,), U8).ap()
        bounds_d = nc.dram_tensor("bounds_d", (NP + 1,), F32).ap()
        seam_max_d = nc.dram_tensor("seam_max_d", (2, D), F32).ap()

        keep = sb("keep", [P, HALF], U8)
        nodes = sb("nodes", [P, NT, 2 * D])
        big = sb("big", [P, NT * 2 * D])
        ab = big[:, :].rearrange("p (c f) -> p c f", c=NT)
        res = sb("res", [P, NT, D])
        G = sb("G", [P, 4, K, 2, D])
        V = sb("V", [P, 2, K, 2, D])
        At = sb("At", [2 * ED, 2, UE])
        So = sb("So", [P, 2, 2 * K * 2 * D])
        afill = sb("afill", [P, 2, UE])
        pre = sb("pre", [P, 2, UE])
        m = sb("m", [P, 2, UE])
        sT = sb("sT", [P, 2, UE])
        idx = sb("idx", [P, 4, 2 * K], I32)
        wij = sb("wij", [D, 2 * D])
        wc = sb("wc", [2 * ED, 2 * D])
        wu = sb("wu", [2 * D, D])
        mb_row = sb("mb_row", [1, 2 * D])
        ub_row = sb("ub_row", [1, D])
        w1_sb = sb("w1_sb", [D, H1])
        w2_sb = sb("w2_sb", [H1, D])
        b1_col = sb("b1_col", [H1, 1])
        b2_row = sb("b2_row", [1, D])
        t_col = sb("t_col", [P, 1])
        ident = sb("ident", [P, P])
        ones = sb("ones", [1, P])
        ones_w = pre[:, 1, 0:ROWS]
        node_i = sb("node_i", [P, NT], I32)
        node_f = sb("node_f", [P, NT])
        row_f = sb("row_f", [P, NT])
        row_i = sb("row_i", [P, NT], I32)
        upto = sb("upto", [P, NT])
        before = sb("before", [P, NT])
        has = sb("has", [P, NT])
        cross = sb("cross", [P, NT])
        tmp = sb("tmp", [P, NT])
        start_i = sb("start_i", [P, NT], I32)
        end_i = sb("end_i", [P, NT], I32)
        seam_part = sb("seam_part", [P, 2])
        seam_all = sb("seam_all", [P, 2])
        seam_i = sb("seam_i", [P, 2], I32)
        seam_row = sb("seam_row", [P, D])
        seam_sum = sb("seam_sum", [P, 2 * D])
        seam_max = G[:, 1].rearrange("p k h f -> p (k h) f")[:, 0:2, :]
        seam_col = sb("seam_col", [D, 1])
        seam_f = G[:, 0].rearrange("p k h f -> p (k h) f")[:, 0:3, :]
        mean = sb("mean", [P, NT])
        var = sb("var", [P, NT])
        std = sb("std", [P, NT])
        zero_col = sb("zero_col", [1, 1])

        psN, psB, psV, psS = ps("psN"), ps("psB"), ps("psV"), ps("psS")

        HB = NT * D
        def run_max(r, a, b):
            return big[:, r * HB + a:r * HB + b]
        def logit(r):
            return big[:, r * HB + 520:r * HB + 520 + UE]
        def expo(r):
            return big[:, r * HB + 1040:r * HB + 1040 + 2 * UE]
        def weighted(r):
            return big[:, r * HB + 2064:r * HB + 2064 + UE]

        psM = psB + psN

        def update_columns(g):
            return V[:, g % 2].rearrange("p k h f -> p (k h f)")

        def table_columns(g):
            return afill[:, g % 2, :]

        def after(i, j):
            return (i, j + 1) if j < 3 else (i + 1, 0)

        def ahead(i, j):
            return (i, j - 1) if j > 0 else (i - 1, 3)

        x_loaded = sem("x_loaded")
        dst_loaded = sem("dst_loaded")
        last_loaded = sem("last_loaded")
        zero_ready = sem("zero_ready")
        cleared = sem("cleared")
        consts_ready = sem("consts_ready")
        ids_ready = sem("ids_ready")
        v_step = sem("v_step")
        rows_found = sem("rows_found")
        row_got = [sem(f"row_got{i}") for i in range(4)]
        row_counted = sem("row_counted")
        upto_ready = sem("upto_ready")
        bounds_stored = sem("bounds_stored")
        bounds_loaded = sem("bounds_loaded")
        seam_parts = sem("seam_parts")
        seam_reduced = sem("seam_reduced")
        index_ready = sem("index_ready")
        keep_ready = sem("keep_ready")
        keep_stored = sem("keep_stored")
        keep_loaded = sem("keep_loaded")
        var_ready = sem("var_ready")
        std_ready = sem("std_ready")
        h_ready = sem("h_ready")
        table_weights_in = sem("table_weights_in")
        edge_weights_in = sem("edge_weights_in")
        upd_weights_in = sem("upd_weights_in")
        mlp_loaded = sem("mlp_loaded")
        tab_turned = sem("tab_turned")
        tab_copied = sem("tab_copied")
        tab_mult = sem("tab_mult")
        ab_ready = sem("ab_ready")
        table_stored = sem("table_stored")
        scattered = sem("scattered")
        seam_got = sem("seam_got")
        seam_stored = sem("seam_stored")
        pool_turn = sem("pool_turn")
        pe_turn = sem("pe_turn")
        dve_turn = sem("dve_turn")
        idx_ready = [sem(f"idx_ready{j}") for j in range(4)]
        gathered = [sem(f"gathered{j}") for j in range(4)]
        attr_ready = [sem(f"attr_ready{j}") for j in range(2)]
        v_ready = [sem(f"v_ready{j}") for j in range(2)]
        v_turned = sem("v_turned")
        b_ready = sem("b_ready")
        filled = sem("filled")
        pre_ready = sem("pre_ready")
        m_ready = sem("m_ready")
        s_ready = sem("s_ready")
        s_turned = sem("s_turned")
        so_ready = sem("so_ready")
        s_stored = [sem(f"s_stored{j}") for j in range(2)]
        reset = sem("reset")
        agg_got = [sem(f"agg_got{g}") for g in range(NG)]
        seam_loaded = sem("seam_loaded")
        seam_spread = sem("seam_spread")
        masked = sem("masked")
        agg_ready = sem("agg_ready")
        upd_turned = sem("upd_turned")
        upd_copied = sem("upd_copied")
        upd_mult = sem("upd_mult")
        upd_done = sem("upd_done")
        msg_ready = sem("msg_ready")
        logit_ready = sem("logit_ready")
        pen_ready = sem("pen_ready")
        carry_ready = sem("carry_ready")
        max_ready = sem("max_ready")
        fall_ready = sem("fall_ready")
        ln_step = sem("ln_step")
        diff_ready = sem("diff_ready")
        exp_ready = sem("exp_ready")
        weighted_ready = sem("weighted_ready")
        den_ready = sem("den_ready")
        max_stored = [sem(f"max_stored{j}") for j in range(2)]
        seam_col_got = sem("seam_col_got")
        seam_cols_stored = sem("seam_cols_stored")
        seam_max_loaded = sem("seam_max_loaded")
        seam_diff = sem("seam_diff")
        seam_exp = sem("seam_exp")
        fin_turned = sem("fin_turned")
        fin_copied = sem("fin_copied")
        fin_hidden = sem("fin_hidden")
        fin_relu = sem("fin_relu")
        fin_mult = sem("fin_mult")
        fin_done = sem("fin_done")
        out_stored = sem("out_stored")

        src_u = src.rearrange("(u p k) -> u p k", p=P, k=2 * K)
        attr_u = attr.rearrange("c (u e) -> u c e", e=UE)
        start_u = start_rows[0:EP, :].rearrange("(h u p k) f -> h u p k f", h=2, p=P, k=K)
        sums_u = sums.rearrange("(h u p k) f -> h u p (k f)", h=2, p=P, k=K)
        numden_u = numden.rearrange("(h u p k) f -> h u p (k f)", h=2, p=P, k=K)
        max_u = maxima.rearrange("f (u e) -> u f e", e=UE)
        clear_v = start_rows.rearrange("(p r) f -> p (r f)", p=P).rearrange("p (a z) -> p a z", z=ZW)
        x_v = x.rearrange("(p c) f -> p c f", p=P)
        out_v = out.rearrange("(p c) f -> p c f", p=P)
        table_v = table.rearrange("(p c) f -> p c f", p=P)

        def by_k(tile, k):
            return tile.rearrange("c (p k) -> c k p", k=K)[:, k, :]

        block = ctx.enter_context(nc.Block())

        @block.sync
        def _(sp):
            sp.dma_start(big[:, 0:KEEP_W].bitcast(I32), dst.rearrange("(p e) -> p e", p=P)).then_inc(dst_loaded, 16)
            sp.dma_start(big[:, 2048:2048 + KEEP_W].bitcast(I32), dst_before.rearrange("(p e) -> p e", p=P)).then_inc(dst_loaded, 16)
            sp.dma_start(pre[:, 0, 0:ROWS].bitcast(I32), dst_last.partition_broadcast(P)).then_inc(last_loaded, 16)
            sp.dma_start(res[:, :, :], x_v).then_inc(x_loaded, 16)
            sp.dma_start(w1_sb[:, :], w1).then_inc(mlp_loaded, 16)
            sp.dma_start(w2_sb[:, :], w2).then_inc(mlp_loaded, 16)
            sp.dma_start(b1_col[:, :], b1.rearrange("(p a) -> p a", a=1)).then_inc(mlp_loaded, 16)
            sp.dma_start(b2_row[:, :], b2.rearrange("(a n) -> a n", a=1)).then_inc(mlp_loaded, 16)
            sp.dma_start(t_col[:, :], t.partition_broadcast(P)).then_inc(mlp_loaded, 16)
            sp.wait_ge(keep_ready, 1)
            sp.dma_start(keep_d.rearrange("(p e) -> p e", p=P), big[:, 4096:4096 + KEEP_W // 4].bitcast(U8)).then_inc(keep_stored, 16)
            sp.wait_ge(keep_stored, 16)
            for h in range(2):
                for q in range(4):
                    a, w = q * (HALF // 4), HALF // 4
                    sp.dma_start(keep[D * h:D * h + D, a:a + w],
                                 keep_d[h * HALF + a:h * HALF + a + w].partition_broadcast(D)).then_inc(keep_loaded, 16)
            sp.wait_ge(v_step, 1)
            sp.dma_start(bounds_d[0:1].rearrange("(a b) -> a b", a=1), zero_col[:, :]).then_inc(bounds_stored, 16)
            sp.wait_ge(upto_ready, 1)
            sp.dma_start(bounds_d[1:NP + 1].rearrange("(p c) -> p c", p=P), upto[:, :]).then_inc(bounds_stored, 16)
            sp.wait_ge(bounds_stored, 32)
            sp.dma_start(before[:, :], bounds_d[0:NP].rearrange("(p c) -> p c", p=P)).then_inc(bounds_loaded, 16)

            def load_idx(w, i, j):
                sp.wait_ge(b_ready, freed(w, 4))
                sp.dma_start(idx[:, j, :], src_u[i * 4 + j]).then_inc(idx_ready[j], 16)

            def table_weights(l):
                sp.dma_start(wij[:, 0:D], msg_w[l, 0:D, :]).then_inc(table_weights_in, 16)
                sp.dma_start(wij[:, D:2 * D], msg_w[l, D:2 * D, :]).then_inc(table_weights_in, 16)
                sp.dma_start(mb_row[:, 0:D], msg_b[bass.ds(l, 1), :]).then_inc(table_weights_in, 16)

            def round_edges(l):
                sp.wait_ge(tab_mult, l * NG + NG)
                sp.dma_start(wc[0:ED, 0:D], msg_w[l, 2 * D:2 * D + ED, :]).then_inc(edge_weights_in, 16)
                sp.dma_start(wc[ED:2 * ED, D:2 * D], msg_w[l, 2 * D:2 * D + ED, :]).then_inc(edge_weights_in, 16)
                sp.dma_start(wu[:, :], upd_w[l, :, :]).then_inc(upd_weights_in, 16)
                sp.dma_start(ub_row[:, :], upd_b[bass.ds(l, 1), :]).then_inc(upd_weights_in, 16)
                if not isinstance(l, int):
                    table_weights(l + 1)
                for g, (c0, n) in enumerate(GROUPS):
                    sp.wait_ge(ab_ready, l * NG + g + 1)
                    sp.dma_start(table_v[:, c0:c0 + n, :], ab[:, c0:c0 + n, D:2 * D]).then_inc(table_stored, 16)
                sp.wait_ge(seam_got, l * 16 + 16)
                sp.dma_start(start_rows[HALF:HALF + 1, :], seam_row[0:1, :]).then_inc(seam_stored, 16)
                with sp.Fori(0, TURNS) as i:
                    for j in range(4):
                        w = (l * TURNS + i) * 4 + j
                        load_idx(w, i, j)
                        sp.wait_ge(b_ready, freed(w, 2))
                        sp.dma_start(At[:, j % 2, :], attr_u[i * 4 + j]).then_inc(attr_ready[j % 2], 16)
                        sp.wait_ge(seam_stored, l * 16 + 16)
                        sp.wait_ge(v_turned, freed(w, 2))
                        for h in range(2):
                            sp.dma_start(V[:, j % 2, :, h, :], start_u[h, i * 4 + j]).then_inc(v_ready[j % 2], 16)
                for r in range(2):
                    sp.wait_ge(s_stored[r], l * (64 * TURNS) + (64 * TURNS + 32))
                sp.dma_start(seam_sum[:, 0:D], sums[HALF - 1, :].partition_broadcast(P)).then_inc(seam_loaded, 16)

            sp.wait_ge(v_step, WEIGHTS_CLEAR)
            table_weights(0)
            with sp.Fori(0, LAYERS - 1) as l:
                round_edges(l)
            round_edges(LAYERS - 1)

            for g, (c0, n) in enumerate(GROUPS):
                sp.wait_ge(msg_ready, g + 1)
                sp.dma_start(table_v[:, c0:c0 + n, :], ab[:, c0:c0 + n, 0:D]).then_inc(table_stored, 16)
            with sp.Fori(0, TURNS) as i:
                for j in range(4):
                    load_idx((i + LAYERS * TURNS) * 4 + j, i, j)
            W = (LAYERS + 1) * UNITS
            for r in range(2):
                sp.wait_ge(s_stored[r], 32 * (1 + W // 2))
                sp.wait_ge(max_stored[r], 16 * (1 + UNITS // 2))
            sp.dma_start(seam_sum[:, :], numden[HALF - 1, :].partition_broadcast(P)).then_inc(seam_loaded, 16)
            column = sp.value_load(seam_i[0:1, 1:2], min_val=0, max_val=HALF - 1)
            sp.dma_start(seam_col[:, :], maxima[:, bass.ds(column, 1)],
                         allow_slow_non_contiguous=True).then_inc(seam_col_got, 16)
            sp.dma_start(seam_max_d[0, :].rearrange("(f a) -> f a", a=1),
                         run_max(1, UE, UE + 1)[0:D, :]).then_inc(seam_cols_stored, 16)
            sp.wait_ge(seam_col_got, 16)
            sp.dma_start(seam_max_d[1, :].rearrange("(f a) -> f a", a=1), seam_col[:, :]).then_inc(seam_cols_stored, 16)
            sp.wait_ge(seam_cols_stored, 32)
            sp.dma_start(seam_max[:, :, :], seam_max_d.partition_broadcast(P)).then_inc(seam_max_loaded, 16)
            for g, (c, n) in enumerate(GROUPS):
                sp.wait_ge(fin_done, g + 1)
                sp.dma_start(out_v[:, c:c + n, :], res[:, c:c + n, :]).then_inc(out_stored, 16)
            sp.wait_ge(out_stored, 16 * NG)

        @block.gpsimd
        def _(pool):
            pool.iota(node_i[:, :], pattern=[[1, NT]], base=0, channel_multiplier=NT).then_inc(ids_ready, 1)
            pool.memset(ident[:, :], 0.0).then_inc(ids_ready, 1)
            pool.wait_ge(ids_ready, 2)
            pool.affine_select(out=ident[:, :], in_=ident[:, :], compare_op=ALU.not_equal, fill=1.0, base=0,
                               pattern=[[-1, P]], channel_multiplier=1).then_inc(consts_ready, 1)

            pool.wait_ge(rows_found, 1)
            dst_rows = dst.rearrange("(a b) -> a b", b=ROW)
            for c in range(NT):
                if c >= 4:
                    pool.wait_ge(row_counted, c - 3)
                pool.indirect_dma_start(
                    out=G[:, c % 4].rearrange("p k h f -> p (k h f)").bitcast(I32), out_offset=None, in_=dst_rows,
                    in_offset=bass.IndirectOffsetOnAxis(ap=row_i[:, c:c + 1], axis=0)).then_inc(row_got[c % 4], 16)
            pool.wait_ge(seam_parts, 1)
            pool.partition_all_reduce(seam_all[:, :], seam_part[:, :], P, bass.bass_isa.ReduceOp.add).then_inc(seam_reduced, 1)
            pool.wait_ge(index_ready, 2)
            pool.wait_ge(cleared, 16 * 2)
            for r in range(2):
                pool.wait_ge(max_stored[r], 16)
                pool.wait_ge(s_stored[r], 32)

            def fetch(w, j):
                pool.wait_ge(idx_ready[j], (w - j) * 4 + 16)
                pool.sem_inc(pool_turn, 1)
                for k in range(K):
                    for h in range(2):
                        pool.indirect_dma_start(
                            out=G[:, j, k, h, :], out_offset=None, in_=table,
                            in_offset=bass.IndirectOffsetOnAxis(ap=idx[:, j, 2 * k + h:2 * k + h + 1], axis=0))\
                            .then_inc(gathered[j], 16)

            def round_edges(l):
                for g, (c0, n) in enumerate(GROUPS):
                    pool.wait_ge(ab_ready, l * NG + g + 1)
                    pool.sem_inc(pool_turn, 1)
                    for c in range(c0, c0 + n):
                        pool.indirect_dma_start(
                            out=start_rows, out_offset=bass.IndirectOffsetOnAxis(ap=start_i[:, c:c + 1], axis=0),
                            in_=ab[:, c, 0:D], in_offset=None).then_inc(scattered, 16)
                pool.wait_ge(scattered, l * (16 * NT) + 16 * NT)
                pool.sem_inc(pool_turn, 1)
                pool.indirect_dma_start(
                    out=seam_row[:, :], out_offset=None, in_=start_rows,
                    in_offset=bass.IndirectOffsetOnAxis(ap=seam_i[:, 0:1], axis=0)).then_inc(seam_got, 16)
                pool.wait_ge(table_stored, l * (16 * NG) + 16 * NG)
                pool.sem_inc(pool_turn, 1)
                with pool.Fori(0, TURNS) as i:
                    for j in range(4):
                        fetch((l * TURNS + i) * 4 + j, j)
                for r in range(2):
                    pool.wait_ge(s_stored[r], l * (64 * TURNS) + (64 * TURNS + 32))
                pool.sem_inc(pool_turn, 1)
                for g, (c0, n) in enumerate(GROUPS):
                    for c in range(c0, c0 + n):
                        pool.indirect_dma_start(
                            out=nodes[:, c, D:2 * D], out_offset=None, in_=sums,
                            in_offset=bass.IndirectOffsetOnAxis(ap=end_i[:, c:c + 1], axis=0)).then_inc(agg_got[g], 16)

            with pool.Fori(0, LAYERS - 1) as l:
                round_edges(l)
            round_edges(LAYERS - 1)
            pool.wait_ge(table_stored, 16 * NG * (LAYERS + 1))
            with pool.Fori(0, TURNS) as i:
                for j in range(4):
                    fetch((i + LAYERS * TURNS) * 4 + j, j)
            W = (LAYERS + 1) * UNITS
            for r in range(2):
                pool.wait_ge(s_stored[r], 32 * (1 + W // 2))
                pool.wait_ge(max_stored[r], 16 * (1 + UNITS // 2))
            pool.wait_ge(seam_cols_stored, 32)
            for g, (c0, n) in enumerate(GROUPS):
                for c in range(c0, c0 + n):
                    pool.indirect_dma_start(
                        out=ab[:, c, :], out_offset=None, in_=numden,
                        in_offset=bass.IndirectOffsetOnAxis(ap=end_i[:, c:c + 1], axis=0)).then_inc(agg_got[g], 16)

        @block.scalar
        def _(act):
            act.wait_ge(zero_ready, 1)
            zeros = So[:, :, :].rearrange("p r f -> p (r f)")[:, 0:ZW].unsqueeze(1)
            for q in range(8):
                s = s_stored[q % 2] if q < 4 else max_stored[q % 2] if q < 6 else cleared
                act.dma_start(clear_v[:, 8 * q:8 * q + 8, :], zeros.broadcast_to([P, 8, ZW])).then_inc(s, 16)
            for s in (m_ready, so_ready, logit_ready, pen_ready, exp_ready):
                act.sem_inc(s, CREDIT)
            act.wait_ge(var_ready, 1)
            nc.scalar.activation(std[:, :], var[:, :], ACT.Sqrt).then_inc(std_ready, 1)

            def columns(turned, copied, bank, tile, base, g, used=None):
                n = GROUPS[g][1]
                rows = D if tile is table_columns else P
                act.wait_ge(turned, base + g + 1)
                if g >= 2:
                    act.wait_ge(used, base + g - 1)
                nc.scalar.activation(tile(g)[0:rows, 0:n * P], bank[g % 2][0:rows, 0:n * P], ACT.Copy).then_inc(copied, 1)

            def store_slot(w, j):
                act.wait_ge(s_stored[j % 2], (w - j) * 16 + 32 * (j // 2) + 32)

            for g in range(NG):
                columns(tab_turned, tab_copied, psV, table_columns, 0, g, tab_mult)

            def round_edges(l):
                with act.Fori(0, TURNS) as i:
                    for j in range(4):
                        w, r = (l * TURNS + i) * 4 + j, j % 2
                        act.wait_ge(pre_ready, done(w))
                        act.wait_ge(s_ready, freed(w, 2))
                        nc.scalar.activation(m[:, r, :], pre[:, r, :], ACT.Relu).then_inc(m_ready, 1)
                        act.wait_ge(s_turned, done(w))
                        store_slot(w, j)
                        rows = So[:, r, 0:2 * K * D].rearrange("p (h k f) -> p k h f", h=2, k=K)
                        nc.scalar.activation(rows, psS[r][:, :].rearrange("p (k h f) -> p k h f", k=K, h=2),
                                             ACT.Copy).then_inc(so_ready, 1)
                        act.wait_ge(so_ready, done(w))
                        for h in range(2):
                            act.dma_start(sums_u[h, i * 4 + j], So[:, r, h * K * D:(h + 1) * K * D]).then_inc(s_stored[r], 16)

            with act.Fori(0, LAYERS - 1) as l:
                round_edges(l)
                for s in range(NG + 2):
                    if s < NG:
                        columns(upd_turned, upd_copied, psN, update_columns, l * NG, s, upd_mult)
                    if s >= 2:
                        columns(tab_turned, tab_copied, psV, table_columns, l * NG + NG, s - 2, tab_mult)
            round_edges(LAYERS - 1)
            for s in range(NG + 1):
                if s < NG:
                    columns(upd_turned, upd_copied, psN, update_columns, (LAYERS - 1) * NG, s, upd_mult)
                if s >= 1:
                    c0, n = GROUPS[s - 1]
                    act.wait_ge(var_ready, s + 1)
                    nc.scalar.activation(std[:, c0:c0 + n], var[:, c0:c0 + n], ACT.Sqrt).then_inc(std_ready, 1)
            act.wait_ge(mlp_loaded, 80)

            def front(i, j):
                v, r = i * 4 + j, j % 2
                act.wait_ge(b_ready, done(v + LAYERS * UNITS))
                act.wait_ge(diff_ready, freed(v, 2))
                nc.scalar.activation(logit(r), psM[j][:, :], ACT.Copy, scale=t_col[:, 0:1]).then_inc(logit_ready, 1)
                nc.scalar.activation(pre[:, r, :], keep[:, bass.ds(v * UE, UE)], ACT.Copy,
                                     scale=FAR, bias=-FAR).then_inc(pen_ready, 1)

            def middle(i, j):
                v, r = i * 4 + j, j % 2
                act.wait_ge(diff_ready, done(v))
                nc.scalar.activation(expo(r), expo(r), ACT.Exp).then_inc(exp_ready, 1)
                act.wait_ge(max_ready, done(v))
                act.dma_start(max_u[v], run_max(r, 1, UE + 1)[D:2 * D, :]).then_inc(max_stored[r], 16)

            def back(i, j):
                v, r = i * 4 + j, j % 2
                w = v + LAYERS * UNITS
                act.wait_ge(s_turned, done(w))
                store_slot(w, j)
                rows = So[:, r, :].rearrange("p (h k q f) -> p q k h f", h=2, k=K, q=2)
                for q, bank in ((0, psS[r]), (1, psV[r])):
                    ins = nc.scalar.activation(rows[:, q], bank[:, :].rearrange("p (k h f) -> p k h f", k=K, h=2), ACT.Copy)
                ins.then_inc(so_ready, 1)
                act.wait_ge(so_ready, done(w))
                for h in range(2):
                    act.dma_start(numden_u[h, v], So[:, r, h * K * 2 * D:(h + 1) * K * 2 * D]).then_inc(s_stored[r], 16)

            def turn(i, first=False, last=False):
                for j in range(4):
                    if not (last and j == 3):
                        front(*after(i, j))
                    middle(i, j)
                    if not (first and j == 0):
                        back(*ahead(i, j))

            front(0, 0)
            turn(0, first=True)
            with act.Fori(1, TURNS - 1) as i:
                turn(i)
            turn(TURNS - 1, last=True)
            back(TURNS - 1, 3)
            act.wait_ge(seam_diff, 1)
            nc.scalar.activation(seam_f[:, 0:2, :], seam_max[:, :, :], ACT.Exp).then_inc(seam_exp, 1)
            for g, (c0, n) in enumerate(GROUPS):
                columns(fin_turned, fin_copied, psN, update_columns, 0, g, fin_hidden)
                act.wait_ge(fin_hidden, g + 1)
                if g >= 2:
                    act.wait_ge(fin_mult, g - 1)
                nc.scalar.activation(m[:, g % 2, 0:n * P], psB[g % 2][:, 0:n * P], ACT.Relu, bias=b1_col[:, 0:1])\
                    .then_inc(fin_relu, 1)

        @block.tensor
        def _(pe):
            for s in (v_turned, b_ready, s_turned):
                pe.sem_inc(s, CREDIT)
            pe.wait_ge(consts_ready, 1)

            def turn_nodes(turned, copied, bank, base, g):
                c0, n = GROUPS[g]
                if g >= 2:
                    pe.wait_ge(copied, base + g - 1)
                for c in range(n):
                    ins = pe.transpose(bank[g % 2][:, c * P:(c + 1) * P], nodes[:, c0 + c, :], ident[:, :])
                ins.then_inc(turned, 1)

            def make_table(base, g):
                pe.wait_ge(tab_copied, base + g + 1)
                if g >= 2:
                    pe.wait_ge(ab_ready, base + g - 1)
                for c in range(GROUPS[g][1]):
                    o = psS[g % 2][:, c * P:(c + 1) * P]
                    pe.matmul(o, table_columns(g)[0:D, c * P:(c + 1) * P], wij[:, :], start=True, stop=False)
                    ins = pe.matmul(o, ones[0:1, :], mb_row[0:1, :], start=False, stop=True)
                ins.then_inc(tab_mult, 1)

            def update(base, g):
                pe.wait_ge(upd_copied, base + g + 1)
                if g >= 2:
                    pe.wait_ge(upd_done, base + g - 1)
                for c in range(GROUPS[g][1]):
                    o = psB[g % 2][:, c * D:(c + 1) * D]
                    pe.matmul(o, update_columns(g)[:, c * P:(c + 1) * P], wu[:, :], start=True, stop=False)
                    ins = pe.matmul(o, ones[0:1, :], ub_row[0:1, :], start=False, stop=True)
                ins.then_inc(upd_mult, 1)

            pe.wait_ge(h_ready, 1)
            pe.wait_ge(v_step, WEIGHTS_CLEAR)
            pe.wait_ge(table_weights_in, 48)
            for s in range(NG + 1):
                if s < NG:
                    turn_nodes(tab_turned, tab_copied, psV, 0, s)
                if s >= 1:
                    make_table(0, s - 1)

            def round_edges(l):
                pe.wait_ge(edge_weights_in, l * 32 + 32)
                pe.wait_ge(ab_ready, l * NG + NG)
                pe.sem_inc(pe_turn, 1)
                with pe.Fori(0, TURNS) as i:
                    for j in range(4):
                        w, r = (l * TURNS + i) * 4 + j, j % 2
                        pe.wait_ge(v_ready[r], (w - j) * 16 + 32 * (j // 2) + 32)
                        pe.wait_ge(filled, freed(w, 2))
                        for k in range(K):
                            ins = pe.transpose(by_k(psV[r][:, :], k), V[:, r, k].rearrange("p h f -> p (h f)"), ident[:, :])
                        ins.then_inc(v_turned, 1)
                        pe.wait_ge(attr_ready[r], (w - j) * 8 + 16 * (j // 2) + 16)
                        pe.wait_ge(pre_ready, freed(w, 2))
                        pe.matmul(psB[r][:, :], wc[:, :], At[:, r, :], start=True, stop=False)
                        pe.wait_ge(gathered[j], (w - j) * 32 + 128)
                        for k in range(K):
                            ins = pe.matmul(by_k(psB[r][:, :], k), G[:, j, k].rearrange("p h f -> p (h f)"), ident[:, :],
                                            start=False, stop=(k == K - 1))
                        ins.then_inc(b_ready, 1)
                        pe.wait_ge(s_ready, done(w))
                        pe.wait_ge(so_ready, freed(w, 2))
                        for k in range(K):
                            ins = pe.transpose(psS[r][:, k * P:(k + 1) * P], by_k(sT[:, r, :], k), ident[:, :])
                        ins.then_inc(s_turned, 1)

            with pe.Fori(0, LAYERS - 1) as l:
                round_edges(l)
                for s in range(NG + 3):
                    if s < NG:
                        pe.wait_ge(agg_ready, l * NG + s + 1)
                        turn_nodes(upd_turned, upd_copied, psN, l * NG, s)
                    if s == 1:
                        pe.wait_ge(upd_weights_in, l * 32 + 32)
                        pe.wait_ge(table_weights_in, l * 48 + 96)
                    if 1 <= s < NG + 1:
                        update(l * NG, s - 1)
                    if 2 <= s < NG + 2:
                        pe.wait_ge(upd_done, l * NG + s - 1)
                        turn_nodes(tab_turned, tab_copied, psV, l * NG + NG, s - 2)
                    if s >= 3:
                        make_table(l * NG + NG, s - 3)
            round_edges(LAYERS - 1)
            pe.wait_ge(upd_weights_in, LAYERS * 32)
            for s in range(NG + 1):
                if s < NG:
                    pe.wait_ge(agg_ready, (LAYERS - 1) * NG + s + 1)
                    turn_nodes(upd_turned, upd_copied, psN, (LAYERS - 1) * NG, s)
                if s >= 1:
                    update((LAYERS - 1) * NG, s - 1)
            pe.wait_ge(upd_done, LAYERS * NG)

            def front(i, j):
                v = i * 4 + j
                pe.wait_ge(gathered[j], i * 128 + (LAYERS * TURNS * 128 + 128))
                pe.wait_ge(weighted_ready, freed(v, 4))
                pe.wait_ge(logit_ready, freed(v, 4))
                for k in range(K):
                    ins = pe.transpose(by_k(psM[j][:, :], k), G[:, j, k].rearrange("p h f -> p (h f)"), ident[:, :])
                ins.then_inc(b_ready, 1)

            def back(i, j):
                w, r = i * 4 + j + LAYERS * UNITS, j % 2
                pe.wait_ge(s_ready, done(w))
                pe.wait_ge(so_ready, freed(w, 2))
                for tile, bank in ((sT, psS[r]), (afill, psV[r])):
                    for k in range(K):
                        ins = pe.transpose(bank[:, k * P:(k + 1) * P], by_k(tile[:, r, :], k), ident[:, :])
                ins.then_inc(s_turned, 1)

            def turn(i, last=False):
                for j in range(4):
                    if not (last and j == 3):
                        front(*after(i, j))
                    back(i, j)

            front(0, 0)
            with pe.Fori(0, TURNS - 1) as i:
                turn(i)
            turn(TURNS - 1, last=True)
            pe.wait_ge(mlp_loaded, 80)
            for g, (c0, n) in enumerate(GROUPS):
                if g == 0:
                    pe.wait_ge(agg_ready, LAYERS * NG + 1)
                    turn_nodes(fin_turned, fin_copied, psN, 0, 0)
                if g + 1 < NG:
                    pe.wait_ge(agg_ready, LAYERS * NG + g + 2)
                    turn_nodes(fin_turned, fin_copied, psN, 0, g + 1)
                pe.wait_ge(fin_copied, g + 1)
                if g >= 2:
                    pe.wait_ge(fin_relu, g - 1)
                pe.matmul(psB[g % 2][:, 0:n * P], w1_sb[:, :], update_columns(g)[0:D, 0:n * P], start=True, stop=True)\
                    .then_inc(fin_hidden, 1)
                pe.wait_ge(fin_relu, g + 1)
                if g >= 2:
                    pe.wait_ge(fin_done, g - 1)
                for c in range(n):
                    o = psV[g % 2][:, c * D:(c + 1) * D]
                    pe.matmul(o, m[:, g % 2, c * P:(c + 1) * P], w2_sb[:, :], start=True, stop=False)
                    ins = pe.matmul(o, ones[0:1, :], b2_row[0:1, :], start=False, stop=True)
                ins.then_inc(fin_mult, 1)

        @block.vector
        def _(dve):
            steps = [0]

            def step(ins):
                steps[0] += 1
                ins.then_inc(v_step, 1)
                dve.wait_ge(v_step, steps[0])

            step(nc.vector.memset(zero_col[:, :], 0.0))
            step(nc.vector.memset(ones[:, :], 1.0))
            step(nc.vector.memset(ones_w, 1.0))
            step(nc.vector.memset(mb_row[:, :], 0.0))
            step(nc.vector.memset(wc[:, :], 0.0))
            nc.vector.memset(So[:, :, :], 0.0).then_inc(zero_ready, 1)
            for s in (filled, pre_ready, s_ready, carry_ready, max_ready, fall_ready, diff_ready, weighted_ready, den_ready):
                dve.sem_inc(s, CREDIT)

            dve.wait_ge(dst_loaded, 32)
            nc.vector.tensor_tensor(big[:, 4096:4096 + KEEP_W // 4].bitcast(U8), big[:, 0:KEEP_W].bitcast(I32),
                                    big[:, 2048:2048 + KEEP_W].bitcast(I32), ALU.is_equal).then_inc(keep_ready, 1)

            dve.wait_ge(ids_ready, 2)
            step(nc.vector.tensor_copy(node_f[:, :], node_i[:, :]))
            dve.wait_ge(last_loaded, 16)
            for c in range(NT):
                ins = nc.vector.scalar_tensor_tensor(
                    out=m[:, 0, 0:ROWS], in0=pre[:, 0, 0:ROWS].bitcast(I32), scalar=node_f[:, c:c + 1], in1=ones_w,
                    op0=ALU.is_le, op1=ALU.mult, accum_out=row_f[:, c:c + 1])
                step(ins)
            step(nc.vector.tensor_scalar(row_f[:, :], row_f[:, :], float(ROWS - 1), None, ALU.min))
            nc.vector.tensor_copy(row_i[:, :], row_f[:, :]).then_inc(rows_found, 1)

            def layer_norm(last):
                def wide(a):
                    return a[:, :].unsqueeze(2).broadcast_to([P, NT, D])
                lo, hi = nodes[:, :, 0:D], nodes[:, :, D:2 * D]
                step(nc.vector.tensor_reduce(mean[:, :], res[:, :, :], AX.X, ALU.add))
                step(nc.vector.tensor_scalar(mean[:, :], mean[:, :], 1.0 / D, None, ALU.mult))
                step(nc.vector.tensor_tensor(lo, res[:, :, :], wide(mean), ALU.subtract))
                step(nc.vector.tensor_tensor(hi, lo, lo, ALU.mult))
                step(nc.vector.tensor_reduce(var[:, :], hi, AX.X, ALU.add))
                nc.vector.tensor_scalar(var[:, :], var[:, :], 1.0 / D, EPS_LN, ALU.mult, ALU.add).then_inc(var_ready, 1)
                dve.wait_ge(std_ready, last)
                step(nc.vector.reciprocal(std[:, :], std[:, :]))
                step(nc.vector.tensor_tensor(lo, lo, wide(std), ALU.mult))
                return nc.vector.tensor_scalar(lo, lo, 0.0, None, ALU.max)

            dve.wait_ge(x_loaded, 16)
            layer_norm(1).then_inc(h_ready, 1)

            step(nc.vector.memset(sT[:, 0, :], 1.0))
            for c in range(NT):
                dve.wait_ge(row_got[c % 4], 16 * (c // 4 + 1))
                if c >= 2:
                    dve.wait_ge(row_counted, c - 1)
                nc.vector.scalar_tensor_tensor(
                    out=m[:, c % 2, :], in0=G[:, c % 4].rearrange("p k h f -> p (k h f)").bitcast(I32),
                    scalar=node_f[:, c:c + 1], in1=sT[:, 0, :],
                    op0=ALU.is_le, op1=ALU.mult, accum_out=upto[:, c:c + 1]).then_inc(row_counted, 1)
            dve.wait_ge(row_counted, NT)
            nc.vector.scalar_tensor_tensor(out=upto[:, :], in0=row_f[:, :], scalar=float(ROW), in1=upto[:, :],
                                           op0=ALU.mult, op1=ALU.add).then_inc(upto_ready, 1)
            dve.wait_ge(bounds_loaded, 16)
            dve.wait_ge(upto_ready, 1)
            tt, ts = nc.vector.tensor_tensor, nc.vector.tensor_scalar
            step(tt(has[:, :], upto[:, :], before[:, :], ALU.is_gt))
            step(ts(tmp[:, :], upto[:, :], -1.0, 0.0, ALU.add, ALU.max))
            step(nc.vector.tensor_copy(end_i[:, :], tmp[:, :]))
            step(ts(tmp[:, :], node_f[:, :], float(EP), None, ALU.add))
            step(tt(mean[:, :], before[:, :], tmp[:, :], ALU.subtract))
            step(tt(mean[:, :], mean[:, :], has[:, :], ALU.mult))
            step(tt(tmp[:, :], mean[:, :], tmp[:, :], ALU.add))
            nc.vector.tensor_copy(start_i[:, :], tmp[:, :]).then_inc(index_ready, 1)
            step(ts(mean[:, :], before[:, :], float(HALF), None, ALU.is_lt))
            step(ts(tmp[:, :], upto[:, :], float(HALF), None, ALU.is_gt))
            step(tt(cross[:, :], mean[:, :], tmp[:, :], ALU.mult))
            step(nc.vector.scalar_tensor_tensor(out=tmp[:, :], in0=before[:, :], scalar=-float(HALF), in1=cross[:, :],
                                                op0=ALU.add, op1=ALU.mult, accum_out=seam_part[:, 0:1]))
            step(nc.vector.scalar_tensor_tensor(out=tmp[:, :], in0=upto[:, :], scalar=-float(HALF + 1), in1=cross[:, :],
                                                op0=ALU.add, op1=ALU.mult, accum_out=seam_part[:, 1:2]))
            dve.sem_inc(seam_parts, 1)
            dve.wait_ge(seam_reduced, 1)
            step(ts(seam_all[:, 0:1], seam_all[:, 0:1], float(HALF), None, ALU.add))
            nc.vector.tensor_copy(seam_i[:, :], seam_all[:, :]).then_inc(index_ready, 1)

            def tiles(a, c0, n):
                return a[:, c0:c0 + n].unsqueeze(2).broadcast_to([P, n, D])

            def copy_table(base, g):
                c0, n = GROUPS[g]
                dve.wait_ge(tab_mult, base + g + 1)
                nc.vector.tensor_copy(ab[:, c0:c0 + n, :], psS[g % 2][:, 0:n * P].rearrange("p (c f) -> p c f", c=n))\
                    .then_inc(ab_ready, 1)

            def round_edges(l):
                nc.vector.memset(afill[:, 1, UE - 1:UE], 0.0).then_inc(reset, 1)
                nc.vector.memset(sT[:, 1, UE - 1:UE], 0.0).then_inc(reset, 1)
                dve.wait_ge(keep_loaded, 128)
                dve.wait_ge(reset, l * 2 + 2)
                dve.sem_inc(dve_turn, 1)
                with dve.Fori(0, TURNS) as i:
                    for j in range(4):
                        w, r = (l * TURNS + i) * 4 + j, j % 2
                        kept = keep[:, bass.ds((i * 4 + j) * UE, UE)]
                        dve.wait_ge(v_turned, done(w))
                        nc.vector.tensor_tensor_scan(afill[:, r, :], kept, psV[r][:, :], afill[:, 1 - r, UE - 1:UE],
                                                     ALU.mult, ALU.add).then_inc(filled, 1)
                        dve.wait_ge(filled, done(w))
                        dve.wait_ge(b_ready, done(w))
                        nc.vector.tensor_tensor(pre[:, r, :], afill[:, r, :], psB[r][:, :], ALU.add).then_inc(pre_ready, 1)
                        dve.wait_ge(m_ready, done(w))
                        dve.wait_ge(s_turned, freed(w, 2))
                        nc.vector.tensor_tensor_scan(sT[:, r, :], kept, m[:, r, :], sT[:, 1 - r, UE - 1:UE],
                                                     ALU.mult, ALU.add).then_inc(s_ready, 1)
                        dve.wait_ge(s_ready, done(w))
                dve.wait_ge(seam_loaded, l * 16 + 16)
                nc.vector.tensor_tensor(ab[:, :, 0:D], tiles(cross, 0, NT),
                                        seam_sum[:, 0:D].unsqueeze(1).broadcast_to([P, NT, D]), ALU.mult).then_inc(seam_spread, 1)
                dve.wait_ge(seam_spread, l + 1)

            def take_sums(l, g):
                c0, n = GROUPS[g]
                agg = nodes[:, c0:c0 + n, D:2 * D]
                dve.wait_ge(agg_got[g], l * (16 * n) + 16 * n)
                tt(agg, agg, tiles(has, c0, n), ALU.mult).then_inc(masked, 1)
                dve.wait_ge(masked, l * NG + g + 1)
                tt(agg, agg, ab[:, c0:c0 + n, 0:D], ALU.add).then_inc(agg_ready, 1)

            def relu_update(l, g):
                c0, n = GROUPS[g]
                dve.wait_ge(upd_mult, l * NG + g + 1)
                ts(nodes[:, c0:c0 + n, 0:D], psB[g % 2][:, 0:n * D].rearrange("p (c f) -> p c f", c=n), 0.0, None,
                   ALU.max).then_inc(upd_done, 1)

            for g in range(NG):
                copy_table(0, g)
            with dve.Fori(0, LAYERS - 1) as l:
                round_edges(l)
                for s in range(NG + 3):
                    if s < NG:
                        take_sums(l, s)
                    if 1 <= s < NG + 1:
                        relu_update(l, s - 1)
                    if s >= 3:
                        copy_table(l * NG + NG, s - 3)
            round_edges(LAYERS - 1)

            def norm_start(g):
                c0, n = GROUPS[g]
                rg, lo, hi = res[:, c0:c0 + n, :], nodes[:, c0:c0 + n, 0:D], nodes[:, c0:c0 + n, D:2 * D]
                mg, vg = mean[:, c0:c0 + n], var[:, c0:c0 + n]
                dve.wait_ge(upd_done, (LAYERS - 1) * NG + g + 1)
                step(tt(rg, rg, lo, ALU.add))
                step(nc.vector.tensor_reduce(mg, rg, AX.X, ALU.add))
                step(ts(mg, mg, 1.0 / D, None, ALU.mult))
                step(tt(lo, rg, tiles(mean, c0, n), ALU.subtract))
                step(tt(hi, lo, lo, ALU.mult))
                step(nc.vector.tensor_reduce(vg, hi, AX.X, ALU.add))
                ts(vg, vg, 1.0 / D, EPS_LN, ALU.mult, ALU.add).then_inc(var_ready, 1)

            def norm_end(g):
                c0, n = GROUPS[g]
                lo = nodes[:, c0:c0 + n, 0:D]
                dve.wait_ge(std_ready, g + 2)
                step(nc.vector.reciprocal(std[:, c0:c0 + n], std[:, c0:c0 + n]))
                step(tt(lo, lo, tiles(std, c0, n), ALU.mult))
                ts(ab[:, c0:c0 + n, 0:D], lo, 0.0, EPS_MSG, ALU.max, ALU.add).then_inc(msg_ready, 1)
                dve.wait_ge(msg_ready, g + 1)
                step(ts(lo, lo, 0.0, None, ALU.max))

            for s in range(NG + 2):
                if s < NG:
                    take_sums(LAYERS - 1, s)
                if 1 <= s < NG + 1:
                    relu_update(LAYERS - 1, s - 1)
                    norm_start(s - 1)
                if s >= 2:
                    norm_end(s - 2)

            dve.wait_ge(table_stored, 16 * NG * (LAYERS + 1))
            step(nc.vector.memset(run_max(1, UE, UE + 1), -FAR))
            step(nc.vector.memset(sT[:, 1, UE - 1:UE], 0.0))
            step(nc.vector.memset(afill[:, 1, UE - 1:UE], 0.0))

            def front(i, j):
                v, r = i * 4 + j, j % 2
                dve.wait_ge(max_stored[r], i * 32 + 16 * (j // 2) + 16)
                nc.vector.tensor_copy(run_max(r, 0, 1), run_max(1 - r, UE, UE + 1)).then_inc(carry_ready, 1)
                dve.wait_ge(carry_ready, done(v))
                dve.wait_ge(logit_ready, done(v))
                dve.wait_ge(pen_ready, done(v))
                nc.vector.tensor_tensor_scan(run_max(r, 1, UE + 1), pre[:, r, :], logit(r), run_max(r, 0, 1),
                                             ALU.add, ALU.max).then_inc(max_ready, 1)
                dve.wait_ge(max_ready, done(v))
                tt(expo(r)[:, 0:UE], run_max(r, 0, UE), run_max(r, 1, UE + 1), ALU.subtract).then_inc(fall_ready, 1)
                tt(expo(r)[:, UE:2 * UE], logit(r), run_max(r, 1, UE + 1), ALU.subtract)
                dve.wait_ge(fall_ready, done(v))
                tt(expo(r)[:, 0:UE], expo(r)[:, 0:UE], pre[:, r, :], ALU.add).then_inc(diff_ready, 1)

            def back(i, j):
                v, r = i * 4 + j, j % 2
                w = v + LAYERS * UNITS
                dve.wait_ge(exp_ready, done(v))
                tt(weighted(r), expo(r)[:, UE:2 * UE], psM[j][:, :], ALU.mult).then_inc(weighted_ready, 1)
                dve.wait_ge(s_turned, freed(w, 2))
                nc.vector.tensor_tensor_scan(afill[:, r, :], expo(r)[:, 0:UE], expo(r)[:, UE:2 * UE],
                                             afill[:, 1 - r, UE - 1:UE], ALU.mult, ALU.add).then_inc(den_ready, 1)
                dve.wait_ge(weighted_ready, done(v))
                nc.vector.tensor_tensor_scan(sT[:, r, :], expo(r)[:, 0:UE], weighted(r),
                                             sT[:, 1 - r, UE - 1:UE], ALU.mult, ALU.add).then_inc(s_ready, 1)
                dve.wait_ge(den_ready, done(v))
                dve.wait_ge(s_ready, done(w))

            def turn(i, last=False):
                for j in range(4):
                    if not (last and j == 3):
                        front(*after(i, j))
                    back(i, j)

            front(0, 0)
            with dve.Fori(0, TURNS - 1) as i:
                turn(i)
            turn(TURNS - 1, last=True)

            dve.wait_ge(seam_max_loaded, 16)
            step(tt(seam_f[:, 2, :], seam_max[:, 0, :], seam_max[:, 1, :], ALU.max))
            tt(seam_max[:, :, :], seam_max[:, :, :], seam_f[:, 2, :].unsqueeze(1).broadcast_to([P, 2, D]),
               ALU.subtract).then_inc(seam_diff, 1)
            dve.wait_ge(seam_exp, 1)
            dve.wait_ge(seam_loaded, 16 * (LAYERS + 1))
            step(tt(seam_sum[:, :].rearrange("p (q f) -> p q f", q=2), seam_sum[:, :].rearrange("p (q f) -> p q f", q=2),
                    seam_f[:, 0, :].unsqueeze(1).broadcast_to([P, 2, D]), ALU.mult))
            step(ts(seam_f[:, 1, :], seam_f[:, 1, :], -1.0, None, ALU.add))

            def rows_of(a, n):
                return a.unsqueeze(1).broadcast_to([P, n, D])
            work = sT[:, :, :].rearrange("p r e -> p (r e)")
            for g, (c0, n) in enumerate(GROUPS):
                dve.wait_ge(agg_got[g], LAYERS * 16 * n + 16 * n)
                both = ab[:, c0:c0 + n, :].rearrange("p c (q f) -> p c q f", q=2)
                num, den = ab[:, c0:c0 + n, 0:D], ab[:, c0:c0 + n, D:2 * D]
                f1 = work[:, 0:n * D].rearrange("p (c f) -> p c f", c=n)
                add = work[:, 512:512 + n * 2 * D].rearrange("p (c q f) -> p c q f", c=n, q=2)
                tt(add, cross[:, c0:c0 + n].unsqueeze(2).unsqueeze(3).broadcast_to([P, n, 2, D]),
                   seam_sum[:, :].rearrange("p (q f) -> p q f", q=2).unsqueeze(1).broadcast_to([P, n, 2, D]), ALU.mult)
                step(tt(f1, tiles(cross, c0, n), rows_of(seam_f[:, 1, :], n), ALU.mult))
                step(ts(f1, f1, 1.0, None, ALU.add))
                step(tt(both, both, f1.unsqueeze(2).broadcast_to([P, n, 2, D]), ALU.mult))
                step(tt(both, both, add, ALU.add))
                step(nc.vector.reciprocal(den, den))
                step(tt(num, num, den, ALU.mult))
                step(tt(num, num, tiles(has, c0, n), ALU.mult))
                tt(nodes[:, c0:c0 + n, 0:D], nodes[:, c0:c0 + n, 0:D], num, ALU.add).then_inc(agg_ready, 1)
                if g >= 2:
                    dve.wait_ge(fin_mult, g - 1)
                    tt(res[:, c0 - 8:c0 - 4, :], res[:, c0 - 8:c0 - 4, :],
                       psV[g % 2][:, 0:4 * D].rearrange("p (c f) -> p c f", c=4), ALU.add).then_inc(fin_done, 1)
            for g in range(NG - 2, NG):
                c0, n = GROUPS[g]
                dve.wait_ge(fin_mult, g + 1)
                tt(res[:, c0:c0 + n, :], res[:, c0:c0 + n, :],
                   psV[g % 2][:, 0:n * D].rearrange("p (c f) -> p c f", c=n), ALU.add).then_inc(fin_done, 1)


def kernel(**inputs):
    import numpy as np
    import concourse.bacc as bacc
    from concourse.bass_utils import run_bass_kernel_spmd

    src = np.zeros((EP,), np.int32)
    src[:E] = inputs["src"]
    src = np.ascontiguousarray(src.reshape(2, UNITS, P, K).transpose(1, 2, 3, 0)).reshape(-1)
    dst = np.full((EP,), N, np.int32)
    dst[:E] = inputs["dst"]
    attr = np.zeros((EP, ED), np.float32)
    attr[:E] = inputs["edge_attr_16"]
    attr = np.ascontiguousarray(attr.reshape(2, HALF, ED).transpose(0, 2, 1)).reshape(2 * ED, HALF)
    x = np.zeros((NP, D), np.float32)
    x[:N] = inputs["x"]
    arrays = {
        "x": x, "src": src, "dst": dst, "dst_before": np.concatenate([np.full((1,), -1, np.int32), dst[:-1]]), "dst_last": dst[ROW - 1::ROW], "attr": attr,
        "msg_w": inputs["L0_gnn_msg_w"], "msg_b": inputs["L0_gnn_msg_b"],
        "upd_w": inputs["L0_gnn_upd_w"], "upd_b": inputs["L0_gnn_upd_b"],
        "w1": inputs["L1_gnn_W1"], "b1": inputs["L1_gnn_b1"], "w2": inputs["L1_gnn_W2"],
        "b2": inputs["L1_gnn_b2"], "t": inputs["L1_gnn_t"],
    }
    arrays = {k: np.ascontiguousarray(a) for k, a in arrays.items()}
    nc = bacc.Bacc("TRN2", target_bir_lowering=False, num_devices=1)
    args = [nc.dram_tensor(k, a.shape, mybir.dt.from_np(a.dtype), kind="ExternalInput").ap() for k, a in arrays.items()]
    out = nc.dram_tensor("out", (NP, D), F32, kind="ExternalOutput").ap()
    build(nc, *args, out)
    r = run_bass_kernel_spmd(nc, [arrays], core_ids=[0])
    return r.results[0]["out"][:N]
```

```python
from contextlib import ExitStack

import concourse.bass as bass
from concourse import mybir

P = 128
N = 6250
D = 64
ED = 16
E = 200000
LAYERS = 3
H1 = 128
NT = -(-N // P)
NP = NT * P
K = 4
UE = P * K
TURNS = -(-E // (2 * UE * 4))
UNITS = 4 * TURNS
HALF = UNITS * UE
EP = 2 * HALF
ROW = 256
ROWS = EP // ROW
KEEP_W = EP // P
GROUPS = [(c, min(4, NT - c)) for c in range(0, NT, 4)]
NG = len(GROUPS)
START_ROWS = EP + NP
ZW = START_ROWS * D // P // 64
CLEARS = 32
FIRST_COPY = 16
assert FIRST_COPY + NG <= CLEARS and 3 * NG <= NT
EPS_LN = 1e-5
EPS_MSG = 1e-7
FAR = 1.0e38
WEIGHTS_CLEAR = 4
CREDIT = 4

F32 = mybir.dt.float32
I32 = mybir.dt.int32
U8 = mybir.dt.uint8
ALU = mybir.AluOpType
ACT = mybir.ActivationFunctionType
AX = mybir.AxisListType
assert START_ROWS * D == P * 64 * ZW and ZW <= 2 * 2 * K * 2 * D


def done(w):
    return w + 1 + CREDIT


def freed(w, slots):
    return w - slots + 1 + CREDIT


def build(nc, x, src, dst, dst_before, dst_last, attr, msg_w, msg_b, upd_w, upd_b, w1, b1, w2, b2, t, out):
    with ExitStack() as ctx:
        def sb(name, shape, dt=F32):
            return ctx.enter_context(nc.sbuf_tensor(name, shape, dt))

        def ps(name):
            return [ctx.enter_context(nc.psum_tensor(f"{name}{i}", [P, 512], F32)) for i in range(2)]

        def sem(name):
            return ctx.enter_context(nc.semaphore(name))

        table = nc.dram_tensor("table", (NP, D), F32).ap()
        start_rows = nc.dram_tensor("start_rows", (START_ROWS, D), F32).ap()
        sums = nc.dram_tensor("sums", (EP, D), F32).ap()
        numden = nc.dram_tensor("numden", (EP, 2 * D), F32).ap()
        maxima = nc.dram_tensor("maxima", (2 * D, HALF), F32).ap()
        keep_d = nc.dram_tensor("keep_d", (EP,), U8).ap()
        bounds_d = nc.dram_tensor("bounds_d", (NP + 1,), F32).ap()

        keep = sb("keep", [P, HALF], U8)
        nodes = sb("nodes", [P, NT, 2 * D])
        big = sb("big", [P, NT * 2 * D])
        ab = big[:, :].rearrange("p (c f) -> p c f", c=NT)
        res = sb("res", [P, NT, D])
        G = sb("G", [P, 4, K, 2, D])
        V = sb("V", [P, 2, K, 2, D])
        At = sb("At", [2 * ED, 2, UE])
        So = sb("So", [P, 2, 2 * K * 2 * D])
        afill = sb("afill", [P, 2, UE])
        pre = sb("pre", [P, 2, UE])
        m = sb("m", [P, 2, UE])
        sT = sb("sT", [P, 2, UE])
        idx = sb("idx", [P, 4, 2 * K], I32)
        wtab = sb("wtab", [D, 3 * D])
        wc = sb("wc", [2 * ED, 2 * D])
        wu = sb("wu", [2 * D, D])
        mb_all = sb("mb_all", [P, 2 * D])
        ub_col = sb("ub_col", [D, 1])
        w1_sb = sb("w1_sb", [D, H1])
        w2_sb = sb("w2_sb", [H1, D])
        b1_col = sb("b1_col", [H1, 1])
        b2_all = sb("b2_all", [P, D])
        t_col = sb("t_col", [P, 1])
        ident = sb("ident", [P, P])

        def row_wide(tile):
            return tile[:, :, :].rearrange("p r e -> p (r e)")[:, 0:ROWS]
        node_i = sb("node_i", [P, NT], I32)
        node_f = sb("node_f", [P, NT])
        row_f = sb("row_f", [P, NT])
        row_i = sb("row_i", [P, NT], I32)
        upto = sb("upto", [P, NT])
        before = sb("before", [P, NT])
        has = sb("has", [P, NT])
        cross = sb("cross", [P, NT])
        tmp = sb("tmp", [P, NT])
        start_i = sb("start_i", [P, NT], I32)
        end_i = sb("end_i", [P, NT], I32)
        seam_part = sb("seam_part", [P, 3])
        seam_all = sb("seam_all", [P, 3])
        seam_i = sb("seam_i", [P, 3], I32)
        seam_row = sb("seam_row", [P, D])
        seam_sum = sb("seam_sum", [P, D])
        seam_part0, seam_part1, seam_max, seam_f = (
            G[0:1, j].rearrange("p k h f -> p (k h) f")[:, 0:2, :] for j in range(4))
        mean = sb("mean", [P, NT])
        var = sb("var", [P, NT])
        std = sb("std", [P, NT])
        zero_col = sb("zero_col", [1, 1])

        psN, psB, psV, psS = ps("psN"), ps("psB"), ps("psV"), ps("psS")

        HB = NT * D
        def run_max(r, a, b):
            return big[:, r * HB + a:r * HB + b]
        def logit(r):
            return big[:, r * HB + 520:r * HB + 520 + UE]
        def expo(r):
            return big[:, r * HB + 1040:r * HB + 1040 + 2 * UE]
        def weighted(r):
            return big[:, r * HB + 2064:r * HB + 2064 + UE]

        psM = psB + psN

        def update_columns(g):
            return V[:, g % 2].rearrange("p k h f -> p (k h f)")

        def table_columns(g):
            return afill[:, g % 2, :]

        def table_bank(g, c):
            return (psS, psV)[c // 2][g % 2]

        def after(i, j):
            return (i, j + 1) if j < 3 else (i + 1, 0)

        def ahead(i, j):
            return (i, j - 1) if j > 0 else (i - 1, 3)

        x_loaded = sem("x_loaded")
        dst_loaded = sem("dst_loaded")
        last_loaded = sem("last_loaded")
        zero_ready = sem("zero_ready")
        cleared = [sem(f"cleared{q}") for q in range(3)]
        consts_ready = sem("consts_ready")
        ids_ready = sem("ids_ready")
        v_step = sem("v_step")
        rows_found = sem("rows_found")
        row_got = [sem(f"row_got{i}") for i in range(4)]
        row_counted = sem("row_counted")
        upto_ready = sem("upto_ready")
        bounds_stored = sem("bounds_stored")
        bounds_loaded = sem("bounds_loaded")
        seam_parts = sem("seam_parts")
        seam_reduced = sem("seam_reduced")
        index_ready = sem("index_ready")
        keep_ready = sem("keep_ready")
        keep_stored = sem("keep_stored")
        keep_loaded = sem("keep_loaded")
        var_ready = sem("var_ready")
        std_ready = sem("std_ready")
        h_ready = sem("h_ready")
        table_weights_in = sem("table_weights_in")
        edge_weights_in = sem("edge_weights_in")
        upd_weights_in = sem("upd_weights_in")
        mlp_loaded = sem("mlp_loaded")
        tab_turned = sem("tab_turned")
        tab_copied = sem("tab_copied")
        tab_mult = sem("tab_mult")
        ab_ready = sem("ab_ready")
        table_stored = sem("table_stored")
        scattered = sem("scattered")
        seam_got = sem("seam_got")
        seam_stored = sem("seam_stored")
        pool_turn = sem("pool_turn")
        pe_turn = sem("pe_turn")
        dve_turn = sem("dve_turn")
        idx_ready = [sem(f"idx_ready{j}") for j in range(4)]
        gathered = [sem(f"gathered{j}") for j in range(4)]
        attr_ready = [sem(f"attr_ready{j}") for j in range(2)]
        v_ready = [sem(f"v_ready{j}") for j in range(2)]
        v_turned = sem("v_turned")
        b_ready = sem("b_ready")
        filled = sem("filled")
        pre_ready = sem("pre_ready")
        m_ready = sem("m_ready")
        s_ready = sem("s_ready")
        s_turned = sem("s_turned")
        so_ready = sem("so_ready")
        s_stored = [sem(f"s_stored{j}") for j in range(2)]
        reset = sem("reset")
        agg_got = [sem(f"agg_got{g}") for g in range(NG)]
        seam_loaded = sem("seam_loaded")
        seam_spread = sem("seam_spread")
        masked = sem("masked")
        agg_ready = sem("agg_ready")
        upd_turned = sem("upd_turned")
        upd_copied = sem("upd_copied")
        upd_mult = sem("upd_mult")
        x_kept = sem("x_kept")
        identity_copied = sem("identity_copied")
        msg_ready = sem("msg_ready")
        logit_ready = sem("logit_ready")
        pen_ready = sem("pen_ready")
        carry_ready = sem("carry_ready")
        max_ready = sem("max_ready")
        fall_ready = sem("fall_ready")
        diff_ready = sem("diff_ready")
        exp_ready = sem("exp_ready")
        weighted_ready = sem("weighted_ready")
        den_ready = sem("den_ready")
        max_stored = [sem(f"max_stored{j}") for j in range(2)]
        seam_parts_in = sem("seam_parts_in")
        seam_joined = sem("seam_joined")
        seam_patched = sem("seam_patched")
        res_ready = sem("res_ready")
        seam_diff = sem("seam_diff")
        seam_exp = sem("seam_exp")
        fin_turned = sem("fin_turned")
        fin_copied = sem("fin_copied")
        fin_hidden = sem("fin_hidden")
        fin_relu = sem("fin_relu")
        fin_mult = sem("fin_mult")
        fin_done = sem("fin_done")
        out_stored = sem("out_stored")

        first = [s_stored[0], s_stored[1], max_stored[0], s_stored[0], s_stored[1], max_stored[1]]
        clear_marks = []
        for q in range(CLEARS):
            s = first[q] if q < 6 else cleared[q % 3]
            clear_marks.append((s, 16 * (1 + sum(s is a for a, _ in clear_marks))))

        src_u = src.rearrange("(u p k) -> u p k", p=P, k=2 * K)
        attr_u = attr.rearrange("c (u e) -> u c e", e=UE)
        start_u = start_rows[0:EP, :].rearrange("(h u p k) f -> h u p k f", h=2, p=P, k=K)
        sums_u = sums.rearrange("(h u p k) f -> h u p (k f)", h=2, p=P, k=K)
        numden_u = numden.rearrange("(h u p k) f -> h u p (k f)", h=2, p=P, k=K)
        max_u = maxima.rearrange("f (u e) -> u f e", e=UE)
        clear_v = start_rows.rearrange("(p r) f -> p (r f)", p=P).rearrange("p (a z) -> p a z", z=ZW)
        x_v = x.rearrange("(p c) f -> p c f", p=P)
        out_v = out.rearrange("(p c) f -> p c f", p=P)
        table_v = table.rearrange("(p c) f -> p c f", p=P)

        def by_k(tile, k):
            return tile.rearrange("c (p k) -> c k p", k=K)[:, k, :]

        def all_cleared(eng):
            for s, value in clear_marks[2:6] + clear_marks[-3:]:
                eng.wait_ge(s, value)

        block = ctx.enter_context(nc.Block())

        @block.sync
        def _(sp):
            def table_weights(l):
                sp.dma_start(wtab[:, 0:D], msg_w[l, 0:D, :]).then_inc(table_weights_in, 16)
                sp.dma_start(wtab[:, D:2 * D], msg_w[l, D:2 * D, :]).then_inc(table_weights_in, 16)
                sp.dma_start(mb_all[:, 0:D], msg_b[bass.ds(l, 1), :].broadcast_to([P, D])).then_inc(table_weights_in, 16)

            sp.dma_start(big[:, 0:KEEP_W].bitcast(I32), dst.rearrange("(p e) -> p e", p=P)).then_inc(dst_loaded, 16)
            sp.dma_start(big[:, 2048:2048 + KEEP_W].bitcast(I32), dst_before.rearrange("(p e) -> p e", p=P)).then_inc(dst_loaded, 16)
            sp.dma_start(row_wide(pre).bitcast(I32), dst_last.partition_broadcast(P)).then_inc(last_loaded, 16)
            sp.dma_start(res[:, :, :], x_v).then_inc(x_loaded, 16)
            sp.dma_start(w1_sb[:, :], w1).then_inc(mlp_loaded, 16)
            sp.dma_start(w2_sb[:, :], w2).then_inc(mlp_loaded, 16)
            sp.dma_start(b1_col[:, :], b1.rearrange("(p a) -> p a", a=1)).then_inc(mlp_loaded, 16)
            sp.dma_start(b2_all[:, :], b2.partition_broadcast(P)).then_inc(mlp_loaded, 16)
            sp.dma_start(t_col[:, :], t.partition_broadcast(P)).then_inc(mlp_loaded, 16)
            sp.wait_ge(v_step, WEIGHTS_CLEAR)
            table_weights(0)
            sp.wait_ge(keep_ready, 1)
            sp.dma_start(keep_d.rearrange("(p e) -> p e", p=P), big[:, 4096:4096 + KEEP_W // 4].bitcast(U8)).then_inc(keep_stored, 16)
            sp.wait_ge(keep_stored, 16)
            sp.wait_ge(v_step, 1)
            sp.dma_start(bounds_d[0:1].rearrange("(a b) -> a b", a=1), zero_col[:, :]).then_inc(bounds_stored, 16)
            sp.wait_ge(upto_ready, 1)
            sp.dma_start(bounds_d[1:NP + 1].rearrange("(p c) -> p c", p=P), upto[:, :]).then_inc(bounds_stored, 16)
            sp.wait_ge(bounds_stored, 32)
            sp.dma_start(before[:, :], bounds_d[0:NP].rearrange("(p c) -> p c", p=P)).then_inc(bounds_loaded, 16)

            def load_idx(w, i, j):
                sp.wait_ge(b_ready, freed(w, 4))
                sp.dma_start(idx[:, j, :], src_u[i * 4 + j]).then_inc(idx_ready[j], 16)

            def round_edges(l):
                sp.wait_ge(tab_mult, l * NG + NG)
                sp.dma_start(wc[0:ED, 0:D], msg_w[l, 2 * D:2 * D + ED, :]).then_inc(edge_weights_in, 16)
                sp.dma_start(wc[ED:2 * ED, D:2 * D], msg_w[l, 2 * D:2 * D + ED, :]).then_inc(edge_weights_in, 16)
                sp.dma_start(wu[:, :], upd_w[l, :, :]).then_inc(upd_weights_in, 16)
                sp.dma_start(ub_col[:, :], upd_b[bass.ds(l, 1), :].rearrange("a f -> f a")).then_inc(upd_weights_in, 16)
                for g, (c0, n) in enumerate(GROUPS):
                    sp.wait_ge(ab_ready, l * NG + g + 1)
                    sp.dma_start(table_v[:, c0:c0 + n, :], ab[:, c0:c0 + n, D:2 * D]).then_inc(table_stored, 16)
                if not isinstance(l, int):
                    table_weights(l + 1)
                sp.wait_ge(seam_got, l * 16 + 16)
                sp.dma_start(start_rows[HALF:HALF + 1, :], seam_row[0:1, :]).then_inc(seam_stored, 16)
                with sp.Fori(0, TURNS) as i:
                    for j in range(4):
                        w = (l * TURNS + i) * 4 + j
                        load_idx(w, i, j)
                        sp.wait_ge(b_ready, freed(w, 2))
                        sp.dma_start(At[:, j % 2, :], attr_u[i * 4 + j]).then_inc(attr_ready[j % 2], 16)
                        sp.wait_ge(seam_stored, l * 16 + 16)
                        sp.wait_ge(v_turned, freed(w, 2))
                        for h in range(2):
                            sp.dma_start(V[:, j % 2, :, h, :], start_u[h, i * 4 + j]).then_inc(v_ready[j % 2], 16)
                for r in range(2):
                    sp.wait_ge(s_stored[r], l * (64 * TURNS) + (64 * TURNS + 32))
                sp.dma_start(seam_sum[:, :], sums[HALF - 1, :].partition_broadcast(P)).then_inc(seam_loaded, 16)

            all_cleared(sp)
            for h in range(2):
                for q in range(4):
                    a, w = q * (HALF // 4), HALF // 4
                    sp.dma_start(keep[D * h:D * h + D, a:a + w],
                                 keep_d[h * HALF + a:h * HALF + a + w].partition_broadcast(D)).then_inc(keep_loaded, 16)
            with sp.Fori(0, LAYERS - 1) as l:
                round_edges(l)
            round_edges(LAYERS - 1)

            for g, (c0, n) in enumerate(GROUPS):
                sp.wait_ge(msg_ready, g + 1)
                sp.dma_start(table_v[:, c0:c0 + n, :], ab[:, c0:c0 + n, 0:D]).then_inc(table_stored, 16)
            with sp.Fori(0, TURNS) as i:
                for j in range(4):
                    load_idx((i + LAYERS * TURNS) * 4 + j, i, j)
            W = (LAYERS + 1) * UNITS
            for r in range(2):
                sp.wait_ge(s_stored[r], 32 * (1 + W // 2))
                sp.wait_ge(max_stored[r], 16 * (1 + UNITS // 2))
            column = sp.value_load(seam_i[0:1, 1:2], min_val=0, max_val=HALF - 1)
            last_row = numden[HALF:EP, :][bass.ds(column, 1), :].rearrange("a (q f) -> a q f", q=2)
            sp.dma_start(seam_part0, numden[HALF - 1:HALF, :].rearrange("a (q f) -> a q f", q=2)).then_inc(seam_parts_in, 16)
            sp.dma_start(seam_part1, last_row).then_inc(seam_parts_in, 16)
            sp.dma_start(seam_max[:, 0, :], maxima[0:D, HALF - 1:HALF].rearrange("f a -> a f"),
                         allow_slow_non_contiguous=True).then_inc(seam_parts_in, 16)
            sp.dma_start(seam_max[:, 1, :], maxima[D:2 * D, bass.ds(column, 1)].rearrange("f a -> a f"),
                         allow_slow_non_contiguous=True).then_inc(seam_parts_in, 16)
            sp.wait_ge(seam_joined, 1)
            sp.dma_start(last_row, seam_part1).then_inc(seam_patched, 16)
            for g, (c, n) in enumerate(GROUPS):
                sp.wait_ge(fin_done, g + 1)
                sp.dma_start(out_v[:, c:c + n, :], res[:, c:c + n, :]).then_inc(out_stored, 16)
            sp.wait_ge(out_stored, 16 * NG)

        @block.gpsimd
        def _(pool):
            pool.iota(node_i[:, :], pattern=[[1, NT]], base=0, channel_multiplier=NT).then_inc(ids_ready, 1)
            pool.memset(ident[:, :], 0.0).then_inc(ids_ready, 1)
            pool.wait_ge(ids_ready, 2)
            pool.affine_select(out=ident[:, :], in_=ident[:, :], compare_op=ALU.not_equal, fill=1.0, base=0,
                               pattern=[[-1, P]], channel_multiplier=1).then_inc(consts_ready, 1)

            pool.wait_ge(rows_found, 1)
            dst_rows = dst.rearrange("(a b) -> a b", b=ROW)
            for c in range(NT):
                if c >= 4:
                    pool.wait_ge(row_counted, c - 3)
                pool.indirect_dma_start(
                    out=G[:, c % 4].rearrange("p k h f -> p (k h f)")[:, 0:ROW].bitcast(I32), out_offset=None, in_=dst_rows,
                    in_offset=bass.IndirectOffsetOnAxis(ap=row_i[:, c:c + 1], axis=0)).then_inc(row_got[c % 4], 16)
            pool.wait_ge(seam_parts, 1)
            pool.partition_all_reduce(seam_all[:, :], seam_part[:, :], P, bass.bass_isa.ReduceOp.add).then_inc(seam_reduced, 1)
            pool.wait_ge(index_ready, 2)
            all_cleared(pool)

            def fetch(w, j):
                pool.wait_ge(idx_ready[j], (w - j) * 4 + 16)
                pool.sem_inc(pool_turn, 1)
                for k in range(K):
                    for h in range(2):
                        pool.indirect_dma_start(
                            out=G[:, j, k, h, :], out_offset=None, in_=table,
                            in_offset=bass.IndirectOffsetOnAxis(ap=idx[:, j, 2 * k + h:2 * k + h + 1], axis=0))\
                            .then_inc(gathered[j], 16)

            def round_edges(l):
                for g, (c0, n) in enumerate(GROUPS):
                    pool.wait_ge(ab_ready, l * NG + g + 1)
                    pool.sem_inc(pool_turn, 1)
                    for c in range(c0, c0 + n):
                        pool.indirect_dma_start(
                            out=start_rows, out_offset=bass.IndirectOffsetOnAxis(ap=start_i[:, c:c + 1], axis=0),
                            in_=ab[:, c, 0:D], in_offset=None).then_inc(scattered, 16)
                pool.wait_ge(scattered, l * (16 * NT) + 16 * NT)
                pool.sem_inc(pool_turn, 1)
                pool.indirect_dma_start(
                    out=seam_row[:, :], out_offset=None, in_=start_rows,
                    in_offset=bass.IndirectOffsetOnAxis(ap=seam_i[:, 0:1], axis=0)).then_inc(seam_got, 16)
                pool.wait_ge(table_stored, l * (16 * NG) + 16 * NG)
                pool.sem_inc(pool_turn, 1)
                with pool.Fori(0, TURNS) as i:
                    for j in range(4):
                        fetch((l * TURNS + i) * 4 + j, j)
                for r in range(2):
                    pool.wait_ge(s_stored[r], l * (64 * TURNS) + (64 * TURNS + 32))
                pool.sem_inc(pool_turn, 1)
                for g, (c0, n) in enumerate(GROUPS):
                    for c in range(c0, c0 + n):
                        pool.indirect_dma_start(
                            out=nodes[:, c, D:2 * D], out_offset=None, in_=sums,
                            in_offset=bass.IndirectOffsetOnAxis(ap=end_i[:, c:c + 1], axis=0)).then_inc(agg_got[g], 16)

            with pool.Fori(0, LAYERS - 1) as l:
                round_edges(l)
            round_edges(LAYERS - 1)
            pool.wait_ge(table_stored, 16 * NG * (LAYERS + 1))
            with pool.Fori(0, TURNS) as i:
                for j in range(4):
                    fetch((i + LAYERS * TURNS) * 4 + j, j)
            W = (LAYERS + 1) * UNITS
            for r in range(2):
                pool.wait_ge(s_stored[r], 32 * (1 + W // 2))
                pool.wait_ge(max_stored[r], 16 * (1 + UNITS // 2))
            pool.wait_ge(seam_patched, 16)
            for g, (c0, n) in enumerate(GROUPS):
                for c in range(c0, c0 + n):
                    pool.indirect_dma_start(
                        out=ab[:, c, :], out_offset=None, in_=numden,
                        in_offset=bass.IndirectOffsetOnAxis(ap=end_i[:, c:c + 1], axis=0)).then_inc(agg_got[g], 16)

        @block.scalar
        def _(act):
            act.wait_ge(zero_ready, 1)
            act.wait_ge(last_loaded, 16)
            act.wait_ge(dst_loaded, 32)
            act.wait_ge(x_loaded, 16)
            zeros = So[:, :, :].rearrange("p r f -> p (r f)")[:, 0:ZW].unsqueeze(1)
            for s in (m_ready, so_ready, logit_ready, pen_ready, exp_ready):
                act.sem_inc(s, CREDIT)
            def columns(turned, copied, bank, tile, base, g, used=None):
                n = GROUPS[g][1]
                rows = D if tile is table_columns else P
                act.wait_ge(turned, base + g + 1)
                if g >= 2:
                    act.wait_ge(used, base + g - 1)
                nc.scalar.activation(tile(g)[0:rows, 0:n * P], bank[g % 2][0:rows, 0:n * P], ACT.Copy).then_inc(copied, 1)

            def store_slot(w, j):
                act.wait_ge(s_stored[j % 2], (w - j) * 16 + 32 * (j // 2) + 32)

            for q in range(CLEARS):
                if q >= 3:
                    act.wait_ge(*clear_marks[q - 3])
                act.dma_start(clear_v[:, 2 * q:2 * q + 2, :], zeros.broadcast_to([P, 2, ZW])).then_inc(clear_marks[q][0], 16)
                if q == FIRST_COPY - 1:
                    act.wait_ge(var_ready, 1)
                    nc.scalar.activation(std[:, :], var[:, :], ACT.Sqrt).then_inc(std_ready, 1)
                if FIRST_COPY <= q < FIRST_COPY + NG:
                    columns(tab_turned, tab_copied, psN, table_columns, 0, q - FIRST_COPY, tab_mult)

            def round_edges(l):
                with act.Fori(0, TURNS) as i:
                    for j in range(4):
                        w, r = (l * TURNS + i) * 4 + j, j % 2
                        act.wait_ge(pre_ready, done(w))
                        act.wait_ge(s_ready, freed(w, 2))
                        nc.scalar.activation(m[:, r, :], pre[:, r, :], ACT.Relu).then_inc(m_ready, 1)
                        act.wait_ge(s_turned, done(w))
                        store_slot(w, j)
                        rows = So[:, r, 0:2 * K * D].rearrange("p (h k f) -> p k h f", h=2, k=K)
                        nc.scalar.activation(rows, psS[r][:, :].rearrange("p (k h f) -> p k h f", k=K, h=2),
                                             ACT.Copy).then_inc(so_ready, 1)
                        act.wait_ge(so_ready, done(w))
                        for h in range(2):
                            act.dma_start(sums_u[h, i * 4 + j], So[:, r, h * K * D:(h + 1) * K * D]).then_inc(s_stored[r], 16)

            def update_and_table(l, g):
                n = GROUPS[g][1]
                act.wait_ge(upd_mult, l * NG + g + 1)
                if g >= 2:
                    act.wait_ge(tab_mult, l * NG + (NG + g - 1))
                nc.scalar.activation(table_columns(g)[0:D, 0:n * P], psB[g % 2][0:D, 0:n * P], ACT.Relu,
                                     bias=ub_col[:, 0:1]).then_inc(tab_copied, 1)

            def keep_rows(l, g):
                c0, n = GROUPS[g]
                act.wait_ge(ab_ready, l * NG + (NG + g + 1))
                for a in range(0, n, 2):
                    b = min(2, n - a)
                    ins = nc.scalar.activation(
                        nodes[:, c0 + a:c0 + a + b, 0:D],
                        table_bank(g, a)[:, 0:3 * D * b].rearrange("p (c f) -> p c f", c=b)[:, :, 2 * D:3 * D], ACT.Copy)
                ins.then_inc(x_kept, 1)

            with act.Fori(0, LAYERS - 1) as l:
                round_edges(l)
                for s in range(NG + 2):
                    if s < NG:
                        columns(upd_turned, upd_copied, psN, update_columns, l * NG, s, upd_mult)
                    if 1 <= s < NG + 1:
                        update_and_table(l, s - 1)
                    if s >= 2:
                        keep_rows(l, s - 2)
            round_edges(LAYERS - 1)
            for s in range(NG + 2):
                if s < NG:
                    columns(upd_turned, upd_copied, psN, update_columns, (LAYERS - 1) * NG, s, upd_mult)
                if 1 <= s < NG + 1:
                    update_and_table(LAYERS - 1, s - 1)
                if s >= 2:
                    c0, n = GROUPS[s - 2]
                    act.wait_ge(var_ready, s)
                    nc.scalar.activation(std[:, c0:c0 + n], var[:, c0:c0 + n], ACT.Sqrt).then_inc(std_ready, 1)
            act.wait_ge(mlp_loaded, 80)

            def front(i, j):
                v, r = i * 4 + j, j % 2
                act.wait_ge(b_ready, done(v + LAYERS * UNITS))
                act.wait_ge(diff_ready, freed(v, 2))
                nc.scalar.activation(logit(r), psM[j][:, :], ACT.Copy, scale=t_col[:, 0:1]).then_inc(logit_ready, 1)
                nc.scalar.activation(pre[:, r, :], keep[:, bass.ds(v * UE, UE)], ACT.Copy,
                                     scale=FAR, bias=-FAR).then_inc(pen_ready, 1)

            def middle(i, j):
                v, r = i * 4 + j, j % 2
                act.wait_ge(diff_ready, done(v))
                nc.scalar.activation(expo(r), expo(r), ACT.Exp).then_inc(exp_ready, 1)
                act.wait_ge(max_ready, done(v))
                act.dma_start(max_u[v], run_max(r, 1, UE + 1)).then_inc(max_stored[r], 16)

            def back(i, j):
                v, r = i * 4 + j, j % 2
                w = v + LAYERS * UNITS
                act.wait_ge(s_turned, done(w))
                store_slot(w, j)
                rows = So[:, r, :].rearrange("p (h k q f) -> p q k h f", h=2, k=K, q=2)
                for q, bank in ((0, psS[r]), (1, psV[r])):
                    ins = nc.scalar.activation(rows[:, q], bank[:, :].rearrange("p (k h f) -> p k h f", k=K, h=2), ACT.Copy)
                ins.then_inc(so_ready, 1)
                act.wait_ge(so_ready, done(w))
                for h in range(2):
                    act.dma_start(numden_u[h, v], So[:, r, h * K * 2 * D:(h + 1) * K * 2 * D]).then_inc(s_stored[r], 16)

            def turn(i, first=False, last=False):
                for j in range(4):
                    if not (last and j == 3):
                        front(*after(i, j))
                    middle(i, j)
                    if not (first and j == 0):
                        back(*ahead(i, j))

            front(0, 0)
            turn(0, first=True)
            with act.Fori(1, TURNS - 1) as i:
                turn(i)
            turn(TURNS - 1, last=True)
            back(TURNS - 1, 3)
            act.wait_ge(seam_diff, 1)
            nc.scalar.activation(seam_f, seam_max, ACT.Exp).then_inc(seam_exp, 1)
            for g, (c0, n) in enumerate(GROUPS):
                columns(fin_turned, fin_copied, psN, update_columns, 0, g, fin_hidden)
                act.wait_ge(fin_hidden, g + 1)
                if g >= 2:
                    act.wait_ge(fin_mult, g - 1)
                nc.scalar.activation(m[:, g % 2, 0:n * P], psB[g % 2][:, 0:n * P], ACT.Relu, bias=b1_col[:, 0:1])\
                    .then_inc(fin_relu, 1)

        @block.tensor
        def _(pe):
            for s in (v_turned, b_ready, s_turned):
                pe.sem_inc(s, CREDIT)
            pe.wait_ge(consts_ready, 1)

            def turn_nodes(turned, copied, bank, base, g):
                c0, n = GROUPS[g]
                if g >= 2:
                    pe.wait_ge(copied, base + g - 1)
                for c in range(n):
                    ins = pe.transpose(bank[g % 2][:, c * P:(c + 1) * P], nodes[:, c0 + c, :], ident[:, :])
                ins.then_inc(turned, 1)

            def make_table(base, g, last=False):
                pe.wait_ge(tab_copied, base + g + 1)
                if last:
                    if g >= 2:
                        pe.wait_ge(res_ready, g - 1)
                elif g >= 2:
                    pe.wait_ge(ab_ready, base + g - 1)
                    if not isinstance(base, int):
                        pe.wait_ge(x_kept, base + (g - 1 - NG))
                for c in range(GROUPS[g][1]):
                    x_t = table_columns(g)[0:D, c * P:(c + 1) * P]
                    if last:
                        ins = pe.matmul(psS[g % 2][:, c * D:(c + 1) * D], x_t, ident[0:D, 0:D], start=True, stop=True)
                    else:
                        ins = pe.matmul(table_bank(g, c)[:, c % 2 * 3 * D:(c % 2 + 1) * 3 * D], x_t, wtab[:, :],
                                        start=True, stop=True)
                ins.then_inc(tab_mult, 1)

            def update(l, g):
                n = GROUPS[g][1]
                pe.wait_ge(upd_copied, l * NG + g + 1)
                if g >= 2:
                    pe.wait_ge(tab_copied, l * NG + (NG + g - 1))
                pe.matmul(psB[g % 2][0:D, 0:n * P], wu[:, :], update_columns(g)[:, 0:n * P], start=True, stop=True)\
                    .then_inc(upd_mult, 1)

            pe.wait_ge(h_ready, 1)
            pe.wait_ge(table_weights_in, 48)
            pe.wait_ge(identity_copied, 1)
            for s in range(NG + 1):
                if s < NG:
                    turn_nodes(tab_turned, tab_copied, psN, 0, s)
                if s >= 1:
                    make_table(0, s - 1)

            def round_edges(l):
                pe.wait_ge(edge_weights_in, l * 32 + 32)
                pe.wait_ge(ab_ready, l * NG + NG)
                pe.sem_inc(pe_turn, 1)
                with pe.Fori(0, TURNS) as i:
                    for j in range(4):
                        w, r = (l * TURNS + i) * 4 + j, j % 2
                        pe.wait_ge(v_ready[r], (w - j) * 16 + 32 * (j // 2) + 32)
                        pe.wait_ge(filled, freed(w, 2))
                        for k in range(K):
                            ins = pe.transpose(by_k(psV[r][:, :], k), V[:, r, k].rearrange("p h f -> p (h f)"), ident[:, :])
                        ins.then_inc(v_turned, 1)
                        pe.wait_ge(attr_ready[r], (w - j) * 8 + 16 * (j // 2) + 16)
                        pe.wait_ge(pre_ready, freed(w, 2))
                        pe.matmul(psB[r][:, :], wc[:, :], At[:, r, :], start=True, stop=False)
                        pe.wait_ge(gathered[j], (w - j) * 32 + 128)
                        for k in range(K):
                            ins = pe.matmul(by_k(psB[r][:, :], k), G[:, j, k].rearrange("p h f -> p (h f)"), ident[:, :],
                                            start=False, stop=(k == K - 1))
                        ins.then_inc(b_ready, 1)
                        pe.wait_ge(s_ready, done(w))
                        pe.wait_ge(so_ready, freed(w, 2))
                        for k in range(K):
                            ins = pe.transpose(psS[r][:, k * P:(k + 1) * P], by_k(sT[:, r, :], k), ident[:, :])
                        ins.then_inc(s_turned, 1)

            with pe.Fori(0, LAYERS - 1) as l:
                round_edges(l)
                for s in range(NG + 2):
                    if s < NG:
                        pe.wait_ge(agg_ready, l * NG + s + 1)
                        turn_nodes(upd_turned, upd_copied, psN, l * NG, s)
                    if s == 1:
                        pe.wait_ge(upd_weights_in, l * 32 + 32)
                        pe.wait_ge(table_weights_in, l * 48 + 96)
                    if 1 <= s < NG + 1:
                        update(l, s - 1)
                    if s >= 2:
                        make_table(l * NG + NG, s - 2)
                pe.wait_ge(x_kept, l * NG + NG)
                pe.sem_inc(pe_turn, 1)
            round_edges(LAYERS - 1)
            pe.wait_ge(upd_weights_in, LAYERS * 32)
            for s in range(NG + 2):
                if s < NG:
                    pe.wait_ge(agg_ready, (LAYERS - 1) * NG + s + 1)
                    turn_nodes(upd_turned, upd_copied, psN, (LAYERS - 1) * NG, s)
                if 1 <= s < NG + 1:
                    update(LAYERS - 1, s - 1)
                if s >= 2:
                    make_table(LAYERS * NG, s - 2, last=True)
            pe.wait_ge(res_ready, NG)

            def front(i, j):
                v = i * 4 + j
                pe.wait_ge(gathered[j], i * 128 + (LAYERS * TURNS * 128 + 128))
                pe.wait_ge(weighted_ready, freed(v, 4))
                pe.wait_ge(logit_ready, freed(v, 4))
                for k in range(K):
                    ins = pe.transpose(by_k(psM[j][:, :], k), G[:, j, k].rearrange("p h f -> p (h f)"), ident[:, :])
                ins.then_inc(b_ready, 1)

            def back(i, j):
                w, r = i * 4 + j + LAYERS * UNITS, j % 2
                pe.wait_ge(s_ready, done(w))
                pe.wait_ge(so_ready, freed(w, 2))
                for tile, bank in ((sT, psS[r]), (afill, psV[r])):
                    for k in range(K):
                        ins = pe.transpose(bank[:, k * P:(k + 1) * P], by_k(tile[:, r, :], k), ident[:, :])
                ins.then_inc(s_turned, 1)

            def turn(i, last=False):
                for j in range(4):
                    if not (last and j >= 2):
                        front(*after(*after(i, j)))
                    back(i, j)

            front(0, 0)
            front(0, 1)
            with pe.Fori(0, TURNS - 1) as i:
                turn(i)
            turn(TURNS - 1, last=True)
            pe.wait_ge(mlp_loaded, 80)
            def last_product(g):
                pe.wait_ge(fin_relu, g + 1)
                if g >= 2:
                    pe.wait_ge(fin_done, g - 1)
                for c in range(GROUPS[g][1]):
                    ins = pe.matmul(psV[g % 2][:, c * D:(c + 1) * D], m[:, g % 2, c * P:(c + 1) * P], w2_sb[:, :],
                                    start=True, stop=True)
                ins.then_inc(fin_mult, 1)

            for s in range(NG + 2):
                if s < NG:
                    pe.wait_ge(agg_ready, LAYERS * NG + s + 1)
                    turn_nodes(fin_turned, fin_copied, psN, 0, s)
                if 1 <= s < NG + 1:
                    g, n = s - 1, GROUPS[s - 1][1]
                    pe.wait_ge(fin_copied, g + 1)
                    if g >= 2:
                        pe.wait_ge(fin_relu, g - 1)
                    pe.matmul(psB[g % 2][:, 0:n * P], w1_sb[:, :], update_columns(g)[0:D, 0:n * P], start=True, stop=True)\
                        .then_inc(fin_hidden, 1)
                if s >= 2:
                    last_product(s - 2)

        @block.vector
        def _(dve):
            steps = [0]

            def step(ins):
                steps[0] += 1
                ins.then_inc(v_step, 1)
                dve.wait_ge(v_step, steps[0])

            step(nc.vector.memset(zero_col[:, :], 0.0))
            step(nc.vector.memset(sT[:, :, :], 1.0))
            step(nc.vector.memset(mb_all[:, :], 0.0))
            step(nc.vector.memset(wc[:, :], 0.0))
            nc.vector.memset(So[:, :, :], 0.0).then_inc(zero_ready, 1)
            for s in (filled, pre_ready, s_ready, carry_ready, max_ready, fall_ready, diff_ready, weighted_ready, den_ready):
                dve.sem_inc(s, CREDIT)

            dve.wait_ge(dst_loaded, 32)
            nc.vector.tensor_tensor(big[:, 4096:4096 + KEEP_W // 4].bitcast(U8), big[:, 0:KEEP_W].bitcast(I32),
                                    big[:, 2048:2048 + KEEP_W].bitcast(I32), ALU.is_equal).then_inc(keep_ready, 1)

            dve.wait_ge(ids_ready, 2)
            step(nc.vector.tensor_copy(node_f[:, :], node_i[:, :]))
            dve.wait_ge(last_loaded, 16)
            for c in range(NT):
                ins = nc.vector.scalar_tensor_tensor(
                    out=row_wide(m), in0=row_wide(pre).bitcast(I32), scalar=node_f[:, c:c + 1], in1=row_wide(sT),
                    op0=ALU.is_le, op1=ALU.mult, accum_out=row_f[:, c:c + 1])
                step(ins)
            step(nc.vector.tensor_scalar(row_f[:, :], row_f[:, :], float(ROWS - 1), None, ALU.min))
            nc.vector.tensor_copy(row_i[:, :], row_f[:, :]).then_inc(rows_found, 1)

            def layer_norm(last):
                def wide(a):
                    return a[:, :].unsqueeze(2).broadcast_to([P, NT, D])
                lo, hi = nodes[:, :, 0:D], nodes[:, :, D:2 * D]
                step(nc.vector.tensor_reduce(mean[:, :], res[:, :, :], AX.X, ALU.add))
                step(nc.vector.tensor_scalar(mean[:, :], mean[:, :], 1.0 / D, None, ALU.mult))
                step(nc.vector.tensor_tensor(lo, res[:, :, :], wide(mean), ALU.subtract))
                step(nc.vector.tensor_tensor(hi, lo, lo, ALU.mult))
                step(nc.vector.tensor_reduce(var[:, :], hi, AX.X, ALU.add))
                nc.vector.tensor_scalar(var[:, :], var[:, :], 1.0 / D, EPS_LN, ALU.mult, ALU.add).then_inc(var_ready, 1)
                dve.wait_ge(std_ready, last)
                step(nc.vector.reciprocal(std[:, :], std[:, :]))
                step(nc.vector.tensor_tensor(lo, lo, wide(std), ALU.mult))
                return nc.vector.tensor_scalar(lo, lo, 0.0, None, ALU.max)

            dve.wait_ge(consts_ready, 1)
            nc.vector.tensor_copy(wtab[:, 2 * D:3 * D], ident[0:D, 0:D]).then_inc(identity_copied, 1)
            dve.wait_ge(x_loaded, 16)
            layer_norm(1).then_inc(h_ready, 1)

            def copy_table(base, g):
                c0, n = GROUPS[g]
                dve.wait_ge(tab_mult, base + g + 1)
                for a in range(0, n, 2):
                    b = min(2, n - a)
                    ins = nc.vector.tensor_tensor(ab[:, c0 + a:c0 + a + b, :],
                                                  table_bank(g, a)[:, 0:3 * D * b].rearrange("p (c f) -> p c f", c=b)[:, :, 0:2 * D],
                                                  mb_all[:, :].unsqueeze(1).broadcast_to([P, b, 2 * D]), ALU.add)
                ins.then_inc(ab_ready, 1)

            dve.wait_ge(keep_stored, 16)
            for c in range(NT):
                dve.wait_ge(row_got[c % 4], 16 * (c // 4 + 1))
                if c >= 2:
                    dve.wait_ge(row_counted, c - 1)
                nc.vector.scalar_tensor_tensor(
                    out=m[:, c % 2, 0:ROW], in0=G[:, c % 4].rearrange("p k h f -> p (k h f)")[:, 0:ROW].bitcast(I32),
                    scalar=node_f[:, c:c + 1], in1=sT[:, 0, 0:ROW],
                    op0=ALU.is_le, op1=ALU.mult, accum_out=upto[:, c:c + 1]).then_inc(row_counted, 1)
                if c % 3 == 2 and c // 3 < NG:
                    copy_table(0, c // 3)
            dve.wait_ge(row_counted, NT)
            nc.vector.scalar_tensor_tensor(out=upto[:, :], in0=row_f[:, :], scalar=float(ROW), in1=upto[:, :],
                                           op0=ALU.mult, op1=ALU.add).then_inc(upto_ready, 1)
            dve.wait_ge(bounds_loaded, 16)
            dve.wait_ge(upto_ready, 1)
            tt, ts = nc.vector.tensor_tensor, nc.vector.tensor_scalar
            step(tt(has[:, :], upto[:, :], before[:, :], ALU.is_gt))
            step(ts(tmp[:, :], upto[:, :], -1.0, 0.0, ALU.add, ALU.max))
            step(nc.vector.tensor_copy(end_i[:, :], tmp[:, :]))
            step(ts(tmp[:, :], node_f[:, :], float(EP), None, ALU.add))
            step(tt(mean[:, :], before[:, :], tmp[:, :], ALU.subtract))
            step(tt(mean[:, :], mean[:, :], has[:, :], ALU.mult))
            step(tt(tmp[:, :], mean[:, :], tmp[:, :], ALU.add))
            nc.vector.tensor_copy(start_i[:, :], tmp[:, :]).then_inc(index_ready, 1)
            step(ts(mean[:, :], before[:, :], float(HALF), None, ALU.is_lt))
            step(ts(tmp[:, :], upto[:, :], float(HALF), None, ALU.is_gt))
            step(tt(cross[:, :], mean[:, :], tmp[:, :], ALU.mult))
            step(nc.vector.scalar_tensor_tensor(out=tmp[:, :], in0=before[:, :], scalar=-float(HALF), in1=cross[:, :],
                                                op0=ALU.add, op1=ALU.mult, accum_out=seam_part[:, 0:1]))
            step(nc.vector.scalar_tensor_tensor(out=tmp[:, :], in0=upto[:, :], scalar=-float(HALF + 1), in1=cross[:, :],
                                                op0=ALU.add, op1=ALU.mult, accum_out=seam_part[:, 1:2]))
            step(nc.vector.tensor_reduce(seam_part[:, 2:3], cross[:, :], AX.X, ALU.add))
            dve.sem_inc(seam_parts, 1)
            dve.wait_ge(seam_reduced, 1)
            step(ts(seam_all[:, 0:1], seam_all[:, 0:1], float(HALF), None, ALU.add))
            nc.vector.tensor_copy(seam_i[:, :], seam_all[:, :]).then_inc(index_ready, 1)

            def tiles(a, c0, n):
                return a[:, c0:c0 + n].unsqueeze(2).broadcast_to([P, n, D])

            def round_edges(l):
                nc.vector.memset(afill[:, 1, UE - 1:UE], 0.0).then_inc(reset, 1)
                nc.vector.memset(sT[:, 1, UE - 1:UE], 0.0).then_inc(reset, 1)
                dve.wait_ge(keep_loaded, 128)
                dve.wait_ge(reset, l * 2 + 2)
                dve.sem_inc(dve_turn, 1)
                with dve.Fori(0, TURNS) as i:
                    for j in range(4):
                        w, r = (l * TURNS + i) * 4 + j, j % 2
                        kept = keep[:, bass.ds((i * 4 + j) * UE, UE)]
                        dve.wait_ge(v_turned, done(w))
                        nc.vector.tensor_tensor_scan(afill[:, r, :], kept, psV[r][:, :], afill[:, 1 - r, UE - 1:UE],
                                                     ALU.mult, ALU.add).then_inc(filled, 1)
                        dve.wait_ge(filled, done(w))
                        dve.wait_ge(b_ready, done(w))
                        nc.vector.tensor_tensor(pre[:, r, :], afill[:, r, :], psB[r][:, :], ALU.add).then_inc(pre_ready, 1)
                        dve.wait_ge(m_ready, done(w))
                        dve.wait_ge(s_turned, freed(w, 2))
                        nc.vector.tensor_tensor_scan(sT[:, r, :], kept, m[:, r, :], sT[:, 1 - r, UE - 1:UE],
                                                     ALU.mult, ALU.add).then_inc(s_ready, 1)
                        dve.wait_ge(s_ready, done(w))
                dve.wait_ge(seam_loaded, l * 16 + 16)
                nc.vector.tensor_tensor(ab[:, :, 0:D], tiles(cross, 0, NT),
                                        seam_sum[:, :].unsqueeze(1).broadcast_to([P, NT, D]), ALU.mult).then_inc(seam_spread, 1)
                dve.wait_ge(seam_spread, l + 1)

            def take_sums(l, g):
                c0, n = GROUPS[g]
                agg = nodes[:, c0:c0 + n, D:2 * D]
                dve.wait_ge(agg_got[g], l * (16 * n) + 16 * n)
                tt(agg, agg, tiles(has, c0, n), ALU.mult).then_inc(masked, 1)
                dve.wait_ge(masked, l * NG + g + 1)
                tt(agg, agg, ab[:, c0:c0 + n, 0:D], ALU.add).then_inc(agg_ready, 1)

            with dve.Fori(0, LAYERS - 1) as l:
                round_edges(l)
                take_sums(l, 0)
                for s in range(NG + 2):
                    if s + 1 < NG:
                        take_sums(l, s + 1)
                    if s >= 2:
                        copy_table(l * NG + NG, s - 2)
            round_edges(LAYERS - 1)

            def norm_start(g):
                c0, n = GROUPS[g]
                rg, lo, hi = res[:, c0:c0 + n, :], nodes[:, c0:c0 + n, 0:D], nodes[:, c0:c0 + n, D:2 * D]
                mg, vg = mean[:, c0:c0 + n], var[:, c0:c0 + n]
                dve.wait_ge(tab_mult, LAYERS * NG + g + 1)
                tt(rg, rg, psS[g % 2][:, 0:n * D].rearrange("p (c f) -> p c f", c=n), ALU.add).then_inc(res_ready, 1)
                dve.wait_ge(res_ready, g + 1)
                step(nc.vector.tensor_reduce(mg, rg, AX.X, ALU.add))
                step(ts(mg, mg, 1.0 / D, None, ALU.mult))
                step(tt(lo, rg, tiles(mean, c0, n), ALU.subtract))
                step(tt(hi, lo, lo, ALU.mult))
                step(nc.vector.tensor_reduce(vg, hi, AX.X, ALU.add))
                ts(vg, vg, 1.0 / D, EPS_LN, ALU.mult, ALU.add).then_inc(var_ready, 1)

            def norm_end(g):
                c0, n = GROUPS[g]
                lo = nodes[:, c0:c0 + n, 0:D]
                dve.wait_ge(std_ready, g + 2)
                step(nc.vector.reciprocal(std[:, c0:c0 + n], std[:, c0:c0 + n]))
                step(tt(lo, lo, tiles(std, c0, n), ALU.mult))
                ts(ab[:, c0:c0 + n, 0:D], lo, 0.0, EPS_MSG, ALU.max, ALU.add).then_inc(msg_ready, 1)
                dve.wait_ge(msg_ready, g + 1)
                step(ts(lo, lo, 0.0, None, ALU.max))

            take_sums(LAYERS - 1, 0)
            for s in range(NG + 3):
                if s + 1 < NG:
                    take_sums(LAYERS - 1, s + 1)
                if 2 <= s < NG + 2:
                    norm_start(s - 2)
                if s >= 3:
                    norm_end(s - 3)

            dve.wait_ge(table_stored, 16 * NG * (LAYERS + 1))
            step(nc.vector.memset(run_max(1, UE, UE + 1), -FAR))
            step(nc.vector.memset(sT[:, 1, UE - 1:UE], 0.0))
            step(nc.vector.memset(afill[:, 1, UE - 1:UE], 0.0))

            def front(i, j):
                v, r = i * 4 + j, j % 2
                dve.wait_ge(max_stored[r], i * 32 + 16 * (j // 2) + 16)
                nc.vector.tensor_copy(run_max(r, 0, 1), run_max(1 - r, UE, UE + 1)).then_inc(carry_ready, 1)
                dve.wait_ge(carry_ready, done(v))
                dve.wait_ge(logit_ready, done(v))
                dve.wait_ge(pen_ready, done(v))
                nc.vector.tensor_tensor_scan(run_max(r, 1, UE + 1), pre[:, r, :], logit(r), run_max(r, 0, 1),
                                             ALU.add, ALU.max).then_inc(max_ready, 1)
                dve.wait_ge(max_ready, done(v))
                tt(expo(r)[:, 0:UE], run_max(r, 0, UE), run_max(r, 1, UE + 1), ALU.subtract).then_inc(fall_ready, 1)
                tt(expo(r)[:, UE:2 * UE], logit(r), run_max(r, 1, UE + 1), ALU.subtract)
                dve.wait_ge(fall_ready, done(v))
                tt(expo(r)[:, 0:UE], expo(r)[:, 0:UE], pre[:, r, :], ALU.add).then_inc(diff_ready, 1)

            def back(i, j):
                v, r = i * 4 + j, j % 2
                w = v + LAYERS * UNITS
                dve.wait_ge(exp_ready, done(v))
                tt(weighted(r), expo(r)[:, UE:2 * UE], psM[j][:, :], ALU.mult).then_inc(weighted_ready, 1)
                dve.wait_ge(s_turned, freed(w, 2))
                nc.vector.tensor_tensor_scan(afill[:, r, :], expo(r)[:, 0:UE], expo(r)[:, UE:2 * UE],
                                             afill[:, 1 - r, UE - 1:UE], ALU.mult, ALU.add).then_inc(den_ready, 1)
                dve.wait_ge(weighted_ready, done(v))
                nc.vector.tensor_tensor_scan(sT[:, r, :], expo(r)[:, 0:UE], weighted(r),
                                             sT[:, 1 - r, UE - 1:UE], ALU.mult, ALU.add).then_inc(s_ready, 1)
                dve.wait_ge(den_ready, done(v))
                dve.wait_ge(s_ready, done(w))

            def turn(i, last=False):
                for j in range(4):
                    if not (last and j == 3):
                        front(*after(i, j))
                    back(i, j)

            front(0, 0)
            with dve.Fori(0, TURNS - 1) as i:
                turn(i)
            turn(TURNS - 1, last=True)

            dve.wait_ge(mlp_loaded, 80)
            step(tt(res[:, :, :], res[:, :, :], b2_all[:, :].unsqueeze(1).broadcast_to([P, NT, D]), ALU.add))
            dve.wait_ge(seam_parts_in, 64)
            flag = seam_all[0:1, 2:3]
            top = pre[0:1, 0, 0:D].unsqueeze(1)
            step(tt(top, seam_max[:, 0:1, :], seam_max[:, 1:2, :], ALU.max))
            tt(seam_max, seam_max, top.broadcast_to([1, 2, D]), ALU.subtract).then_inc(seam_diff, 1)
            dve.wait_ge(seam_exp, 1)
            step(ts(seam_f[:, 1, :], seam_f[:, 1, :], -1.0, flag, ALU.add, ALU.mult))
            step(ts(seam_f[:, 1, :], seam_f[:, 1, :], 1.0, None, ALU.add))
            step(ts(seam_f[:, 0, :], seam_f[:, 0, :], flag, None, ALU.mult))
            step(tt(seam_part0, seam_part0, seam_f[:, 0:1, :].broadcast_to([1, 2, D]), ALU.mult))
            step(tt(seam_part1, seam_part1, seam_f[:, 1:2, :].broadcast_to([1, 2, D]), ALU.mult))
            tt(seam_part1, seam_part1, seam_part0, ALU.add).then_inc(seam_joined, 1)

            for g, (c0, n) in enumerate(GROUPS):
                dve.wait_ge(agg_got[g], LAYERS * 16 * n + 16 * n)
                num, den = ab[:, c0:c0 + n, 0:D], ab[:, c0:c0 + n, D:2 * D]
                step(nc.vector.reciprocal(den, den))
                step(tt(num, num, den, ALU.mult))
                step(tt(num, num, tiles(has, c0, n), ALU.mult))
                tt(nodes[:, c0:c0 + n, 0:D], nodes[:, c0:c0 + n, 0:D], num, ALU.add).then_inc(agg_ready, 1)
                if g >= 3:
                    dve.wait_ge(fin_mult, g - 2)
                    tt(res[:, c0 - 12:c0 - 8, :], res[:, c0 - 12:c0 - 8, :],
                       psV[(g - 3) % 2][:, 0:4 * D].rearrange("p (c f) -> p c f", c=4), ALU.add).then_inc(fin_done, 1)
            for g in range(NG - 3, NG):
                c0, n = GROUPS[g]
                dve.wait_ge(fin_mult, g + 1)
                tt(res[:, c0:c0 + n, :], res[:, c0:c0 + n, :],
                   psV[g % 2][:, 0:n * D].rearrange("p (c f) -> p c f", c=n), ALU.add).then_inc(fin_done, 1)


def kernel(**inputs):
    import numpy as np
    import concourse.bacc as bacc
    from concourse.bass_utils import run_bass_kernel_spmd

    src = np.zeros((EP,), np.int32)
    src[:E] = inputs["src"]
    src = np.ascontiguousarray(src.reshape(2, UNITS, P, K).transpose(1, 2, 3, 0)).reshape(-1)
    dst = np.full((EP,), N, np.int32)
    dst[:E] = inputs["dst"]
    attr = np.zeros((EP, ED), np.float32)
    attr[:E] = inputs["edge_attr_16"]
    attr = np.ascontiguousarray(attr.reshape(2, HALF, ED).transpose(0, 2, 1)).reshape(2 * ED, HALF)
    x = np.zeros((NP, D), np.float32)
    x[:N] = inputs["x"]
    arrays = {
        "x": x, "src": src, "dst": dst, "dst_before": np.concatenate([np.full((1,), -1, np.int32), dst[:-1]]), "dst_last": dst[ROW - 1::ROW], "attr": attr,
        "msg_w": inputs["L0_gnn_msg_w"], "msg_b": inputs["L0_gnn_msg_b"],
        "upd_w": inputs["L0_gnn_upd_w"], "upd_b": inputs["L0_gnn_upd_b"],
        "w1": inputs["L1_gnn_W1"], "b1": inputs["L1_gnn_b1"], "w2": inputs["L1_gnn_W2"],
        "b2": inputs["L1_gnn_b2"], "t": inputs["L1_gnn_t"],
    }
    arrays = {k: np.ascontiguousarray(a) for k, a in arrays.items()}
    nc = bacc.Bacc("TRN2", target_bir_lowering=False, num_devices=1)
    args = [nc.dram_tensor(k, a.shape, mybir.dt.from_np(a.dtype), kind="ExternalInput").ap() for k, a in arrays.items()]
    out = nc.dram_tensor("out", (NP, D), F32, kind="ExternalOutput").ap()
    build(nc, *args, out)
    r = run_bass_kernel_spmd(nc, [arrays], core_ids=[0])
    return r.results[0]["out"][:N]
```
